# Optimizing a Trainium2 kernel written in Bass

```python
import numpy as np
import jax
import jax.numpy as jnp

def _softmax(x, axis=-1):
    return jax.nn.softmax(x, axis=axis)

def _gelu(x):
    return jax.nn.gelu(x, approximate=True)

def _silu(x):
    return jax.nn.silu(x)

def _sigmoid(x):
    return jax.nn.sigmoid(x)

def _layernorm(x, axis=-1, eps=1e-05):
    m = jnp.mean(x, axis=axis, keepdims=True)
    v = jnp.var(x, axis=axis, keepdims=True)
    return (x - m) / jnp.sqrt(v + eps)

def _scatter_add(tgt, idx, src, axis=0):
    return tgt.at[idx].add(src)

def _segment_sum(src, seg, n):
    return jax.ops.segment_sum(src, seg, n)
kernel_name = 'mk_xattn_ffn_d1_seqx_r4_c583c4'

def setup_inputs(seed: int=0):
    np.random.seed(seed)
    _w = jnp.asarray

    def _rec_inputs():
        import jax
        import jax.numpy as jnp
        _rk = jax.random.key(seed)
        x = -0.0002928 + 1 * jax.random.normal(jax.random.fold_in(_rk, 1), (2, 512, 256), jnp.float32)
        _lenS = 512 - jax.random.randint(jax.random.fold_in(_rk, 7), (2,), 0, max(1, 512 // 4) + 1, jnp.int32)
        _lenS2 = 1024 - jax.random.randint(jax.random.fold_in(_rk, 8), (2,), 0, max(1, 1024 // 4) + 1, jnp.int32)
        _ctx_1024P = jax.random.normal(jax.random.fold_in(_rk, 11), (2, 16, 256), jnp.float32)
        _ctx_1024c = jax.random.dirichlet(jax.random.fold_in(_rk, 511), 0.3 * jnp.ones((16,), jnp.float32), (2, 1024))
        _ctx_1024t = jnp.einsum('bsk,bkd->bsd', _ctx_1024c, _ctx_1024P)
        _ctx_1024t = _ctx_1024t * jax.lax.rsqrt(jnp.mean(jnp.square(_ctx_1024t)) + 1e-12) * 0.953939
        ctx_1024 = -1.39393e-06 + 0.999914 * (_ctx_1024t + 0.3 * jax.random.normal(jax.random.fold_in(_rk, 611), (2, 1024, 256), jnp.float32))
        return (x, ctx_1024)
    x, ctx_1024 = _rec_inputs()

    def _L0_xattn_setup():
        import jax, jax.numpy as jnp
        import numpy as np
        B, S, D, H = (2, 512, 256, 16)
        HD = D // H
        SCALE = HD ** (-0.5)
        NEG = -1000000000.0
        key = jax.random.key(seed)
        ks = jax.random.split(key, 7)
        w_std = 1.0 / np.sqrt(D)
        return {'query': jax.random.normal(ks[0], (B, S, D), dtype=jnp.float32), 'key': jax.random.normal(ks[1], (B, S, D), dtype=jnp.float32), 'value': jax.random.normal(ks[2], (B, S, D), dtype=jnp.float32), 'Wq': jax.random.normal(ks[3], (D, D), dtype=jnp.float32) * w_std, 'Wk': jax.random.normal(ks[4], (D, D), dtype=jnp.float32) * w_std, 'Wv': jax.random.normal(ks[5], (D, D), dtype=jnp.float32) * w_std, 'Wo': jax.random.normal(ks[6], (D, D), dtype=jnp.float32) * w_std}
    _L0_xattn_all = _L0_xattn_setup()
    _L0_xattn_in = {k: v for k, v in _L0_xattn_all.items() if k in ('Wq', 'Wk', 'Wv', 'Wo')}
    del _L0_xattn_all

    def _L0_ffn_setup():
        import jax, jax.numpy as jnp
        import numpy as np
        H = 256
        I = 1024
        E = 4
        LN_EPS = 1e-12

        def _layer_norm(x, gamma, beta, eps=LN_EPS):
            mu = jnp.mean(x, axis=-1, keepdims=True)
            var = jnp.mean(jnp.square(x - mu), axis=-1, keepdims=True)
            return (x - mu) * jax.lax.rsqrt(var + eps) * gamma + beta
        key = jax.random.key(seed)
        ks = jax.random.split(key, 8)
        B, S = (4, 128)
        scale = 0.02
        return {'hidden_states': jax.random.normal(ks[0], (B, S, H), jnp.float32), 'W_router': jax.random.normal(ks[1], (H, E), jnp.float32) * scale, 'W1': jax.random.normal(ks[2], (E, H, I), jnp.float32) * scale, 'b1': jax.random.normal(ks[3], (E, I), jnp.float32) * scale, 'Wo': jax.random.normal(ks[4], (I, H), jnp.float32) * scale, 'bo': jax.random.normal(ks[5], (H,), jnp.float32) * scale, 'ln_gamma': jnp.ones((H,), jnp.float32), 'ln_beta': jnp.zeros((H,), jnp.float32)}
    _L0_ffn_all = _L0_ffn_setup()
    _L0_ffn_in = {k: v for k, v in _L0_ffn_all.items() if k in ('W_router', 'W1', 'b1', 'Wo', 'bo', 'ln_gamma', 'ln_beta')}
    del _L0_ffn_all
    return {'x': x, 'ctx_1024': ctx_1024, 'L0_xattn_Wq': _L0_xattn_in['Wq'], 'L0_xattn_Wk': _L0_xattn_in['Wk'], 'L0_xattn_Wv': _L0_xattn_in['Wv'], 'L0_xattn_Wo': _L0_xattn_in['Wo'], 'L0_ffn_W_router': _L0_ffn_in['W_router'], 'L0_ffn_W1': _L0_ffn_in['W1'], 'L0_ffn_b1': _L0_ffn_in['b1'], 'L0_ffn_Wo': _L0_ffn_in['Wo'], 'L0_ffn_bo': _L0_ffn_in['bo'], 'L0_ffn_ln_gamma': _L0_ffn_in['ln_gamma'], 'L0_ffn_ln_beta': _L0_ffn_in['ln_beta']}

def reference(x, ctx_1024, L0_xattn_Wq, L0_xattn_Wk, L0_xattn_Wv, L0_xattn_Wo, L0_ffn_W_router, L0_ffn_W1, L0_ffn_b1, L0_ffn_Wo, L0_ffn_bo, L0_ffn_ln_gamma, L0_ffn_ln_beta):
    import jax
    import jax.numpy as jnp

    def _L0_xattn_ref(query, key, value, Wq, Wk, Wv, Wo):
        import jax, jax.numpy as jnp
        import numpy as np
        B, S, D, H = (2, 512, 256, 16)
        HD = D // H
        SCALE = HD ** (-0.5)
        NEG = -1000000000.0
        b, sq, d = query.shape
        sk = key.shape[1]
        q = (query @ Wq.T).reshape(b, sq, H, HD).transpose(0, 2, 1, 3)
        k = (key @ Wk.T).reshape(b, sk, H, HD).transpose(0, 2, 1, 3)
        v = (value @ Wv.T).reshape(b, sk, H, HD).transpose(0, 2, 1, 3)
        scores = jnp.einsum('bhqd,bhkd->bhqk', q, k) * SCALE
        causal = jnp.arange(sq)[:, None] >= jnp.arange(sk)[None, :]
        scores = jnp.where(causal[None, None], scores, NEG)
        attn = jax.nn.softmax(scores, axis=-1)
        out = jnp.einsum('bhqk,bhkd->bhqd', attn, v)
        out = out.transpose(0, 2, 1, 3).reshape(b, sq, d)
        return out @ Wo.T

    def _L0_ffn_ref(hidden_states, W_router, W1, b1, Wo, bo, ln_gamma, ln_beta):
        import jax, jax.numpy as jnp
        import numpy as np
        H = 256
        I = 1024
        E = 4
        LN_EPS = 1e-12

        def _layer_norm(x, gamma, beta, eps=LN_EPS):
            mu = jnp.mean(x, axis=-1, keepdims=True)
            var = jnp.mean(jnp.square(x - mu), axis=-1, keepdims=True)
            return (x - mu) * jax.lax.rsqrt(var + eps) * gamma + beta
        B, S, _ = hidden_states.shape
        x = hidden_states.reshape(-1, H)
        logits = x @ W_router
        expert_idx = jnp.argmax(logits, axis=-1)
        h = jnp.einsum('th,ehi->tei', x, W1) + b1
        h = jax.nn.gelu(h, approximate=False)
        onehot = jax.nn.one_hot(expert_idx, E, dtype=x.dtype)
        intermediate = jnp.einsum('te,tei->ti', onehot, h)
        y = intermediate @ Wo + bo + x
        y = _layer_norm(y, ln_gamma, ln_beta)
        return y.reshape(B, S, H)
    x = x + _L0_xattn_ref(_layernorm(x, axis=-1), ctx_1024, ctx_1024, L0_xattn_Wq, L0_xattn_Wk, L0_xattn_Wv, L0_xattn_Wo)
    x = x + _L0_ffn_ref(_layernorm(x, axis=-1), L0_ffn_W_router, L0_ffn_W1, L0_ffn_b1, L0_ffn_Wo, L0_ffn_bo, L0_ffn_ln_gamma, L0_ffn_ln_beta)
    return x

_drawn_inputs = setup_inputs


def setup_inputs(seed=0):
    import zlib

    import numpy as np

    out = dict(_drawn_inputs(seed))
    spreads = {'L0_ffn_ln_gamma': (1.0, 0.2), 'L0_ffn_ln_beta': (0.0, 0.1)}
    factors = {'L0_ffn_b1': 8.0, 'L0_ffn_bo': 5.794}
    for name, (base, spread) in spreads.items():
        noise = np.random.default_rng([zlib.crc32(name.encode()), seed]).standard_normal(out[name].shape)
        drawn = base * np.exp(spread * noise) if base else spread * noise
        out[name] = jnp.asarray(drawn.astype(out[name].dtype))
    for name, factor in factors.items():
        out[name] = (out[name] * factor).astype(out[name].dtype)
    return out
```

```python
import concourse.bass as bass
from concourse import mybir
from contextlib import ExitStack


def cross_attention_moe_ffn(nc: bass.Bass, x, ctxT, wqT, wkT, wvT, woT, w_router, w1, b1, wo, bo, gamma, beta, out):
    fp32, bf16, f32r = mybir.dt.float32, mybir.dt.bfloat16, mybir.dt.float32r
    ALU, ACT = mybir.AluOpType, mybir.ActivationFunctionType

    P = 128
    B, SQ, D = x.shape
    HD = 16
    H = D // HD
    SCALE = HD ** -0.5
    KC = D // P
    QT = SQ // P
    NT = B * QT
    HU = P // HD
    NU = B * KC
    GH = 4
    NG = B * H // GH
    GB = NG // B
    NH = B * H
    E, _, I = w1.shape
    IC = I // P
    LN_EPS, FFN_EPS = 1e-5, 1e-12
    PARTS_Q = (0, 0, 0, 1, 1, 2)
    PARTS_K = (0, 1, 2, 0, 1, 0)
    KROWS = HD * len(PARTS_Q)
    KROWS_M = KROWS + 2
    PCOLS = P * QT * (QT + 1) // 2
    NEG = -1.0e30
    LAG = 8
    AUG = 3
    PR = 8

    ctx = ExitStack()
    with ctx:
        SBUF_BASE = 16512
        place = {"next": SBUF_BASE}

        def width(shape, dt):
            n = mybir.dt.size(dt)
            for d in shape[1:]:
                n *= d
            return -(-n // 32) * 32

        def sb(name, shape, dt=fp32):
            at = place["next"]
            place["next"] = at + width(shape, dt)
            place[name] = at
            return nc.alloc_sbuf_tensor_at(name, shape, dt, offset=at)

        def over(name, shape, dt, first, skip=0):
            return nc.alloc_sbuf_tensor_at(name, shape, dt, offset=place[first] + skip)

        def sem(name):
            return ctx.enter_context(nc.semaphore(name))

        xs = sb("xs", [P, NT, D])
        xn = sb("xn", [P, NT, D])
        xnT = sb("xnT", [P, KC, B * SQ])
        ctxT_s = sb("ctxT_s", [P, KC, B, SQ])
        w1f = over("w1f", [P, 2, E, KC, P], fp32, "ctxT_s")
        wqkv = sb("wqkv", [P, 3, KC, D])
        g_ring = over("g_ring", [P, 2, SQ], fp32, "wqkv")
        wo_att = sb("wo_att", [P, GB, D])
        vaug = sb("vaug", [P, NT, H, 32])
        aug = sb("aug", [P, AUG, 2, HU, SQ], bf16)
        pT = sb("pT", [P, PR, PCOLS])
        split = sb("split", [P, 2, 3, SQ], bf16)
        rest = sb("rest", [P, 2, SQ])
        oT = sb("oT", [P, 2, SQ])
        rec = over("rec", [P, SQ], fp32, "wqkv", 4 * KC * 2 * D)
        onT = sb("onT", [P, GB, SQ])
        w1h = sb("w1h", [P, 2, E, KC, P], f32r)
        w1l = sb("w1l", [P, 2, E, KC, P], f32r)
        wo_s = sb("wo_s", [P, IC, D])
        wr_s = sb("wr_s", [P, KC, E])
        b1f = sb("b1f", [36, I])
        b1s = over("b1s", [36, I], f32r, "rest")
        gam = sb("gam", [P, D])
        bet = sb("bet", [P, D])
        bo_s = sb("bo_s", [P, D])
        mask = sb("mask", [P, SQ], bf16)
        ident = sb("ident", [P, P])
        identb = sb("identb", [P, P], bf16)
        ones_sq = sb("ones_sq", [P, P])
        sel = sb("sel", [P, P])
        mhalf = sb("mhalf", [P, QT])
        mmax = sb("mmax", [P, 2, QT, GH])
        mparts = sb("mparts", [P, 2, QT, 2, GH], bf16)
        mrow = sb("mrow", [2 * GH, 2, SQ], bf16)
        stats = sb("stats", [P, 3, NT, 6])
        mv = sb("mv", [P, 3, NT, 2])
        veps = sb("veps", [P, 3, NT])
        rstd = sb("rstd", [P, 3, NT])
        lg = sb("lg", [P, NT, E])
        lmax = sb("lmax", [P, NT])
        pri = sb("pri", [P, E])
        oh = sb("oh", [P, NT, 36])
        ohT = over("ohT", [36, B * SQ], f32r, "split")

        XB = E * KC * SQ * 4
        xmT = [[over(f"xmT{half}{part}", [P, E, KC, SQ], f32r, first, part * XB) for part in range(2)]
               for half, first in enumerate(("aug", "pT"))]
        xm_s = over("xm_s", [P, 2, E * D], fp32, "aug", 2 * XB)

        ps = ctx.enter_context(nc.psum_tensor("ps", [P, 8, 512], fp32))
        S0, T0, PO, PM = 0, 3, 6, 7

        ld_x = [sem(f"ld_x{b}") for b in range(B)]
        ld_ctx = [sem(f"ld_ctx{b}") for b in range(B)]
        ld_wq, ld_wk, ld_wv = sem("ld_wq"), sem("ld_wk"), sem("ld_wv")
        ld_small = sem("ld_small")
        ld_b1 = sem("ld_b1")
        ld_woT = sem("ld_woT")
        ld_wo = sem("ld_wo")
        ld_w1 = [sem("ld_w1a"), sem("ld_w1b")]
        zeroed = sem("zeroed")
        vzero = sem("vzero")
        stat_done = sem("stat_done")
        veps_done = sem("veps_done")
        rstd_done = sem("rstd_done")
        xn_done = sem("xn_done")
        pre_fill = sem("pre_fill")
        pre_act = sem("pre_act")
        pre_dve = sem("pre_dve")
        mid_done = sem("mid_done")
        low_done = sem("low_done")
        scr_done = [sem("scr_done0"), sem("scr_done1")]
        aug_done = [sem(f"aug_done{s}") for s in range(AUG)]
        s_fill = sem("s_fill")
        s_free = sem("s_free")
        m_done = sem("m_done")
        mh_done = sem("mh_done")
        mdma_done = [sem("mdma_done0"), sem("mdma_done1")]
        t_fill = sem("t_fill")
        t_free = sem("t_free")
        p_masked = sem("p_masked")
        pv_done = sem("pv_done")
        o_done = sem("o_done")
        pm_fill = sem("pm_fill")
        pm_free = sem("pm_free")
        on_done = sem("on_done")
        post_fill = sem("post_fill")
        post_act = sem("post_act")
        post_dve = sem("post_dve")
        oh_step = sem("oh_step")
        xm_done = sem("xm_done")
        b1_done = sem("b1_done")
        w1h_done = sem("w1h_done")
        w1l_done = sem("w1l_done")
        h_fill = sem("h_fill")
        g_done = sem("g_done")
        y_done = sem("y_done")
        xb_done = sem("xb_done")
        fin = sem("fin")
        z_done = sem("z_done")
        out_done = sem("out_done")

        scr = nc.dram_tensor("parts_scratch", (2 * NU, P, 3, SQ), bf16, kind="Internal").ap()

        PRE = []
        for b in range(B):
            PRE += [("xT", b * QT + t) for t in range(QT)]
            PRE += [("qk", 2 * (b * KC + c) + j) for c in range(KC) for j in range(2)]
            PRE += [("v", b * QT + t) for t in range(QT)]
        NPRE = len(PRE)

        def dve_jobs(i):
            return sum(k == "qk" for k, _ in PRE[:i])

        OPEN_JOBS = {GH - 1: [("mT", 0)], LAG - 1: [("mT", 1)]}
        STEPS = NH + 3
        STEP_JOBS = {}
        for n in range(STEPS):
            jobs = []
            g = (n + GH) // GH
            if n % GH == 0 and LAG // GH <= g < NG:
                jobs.append(("mT", g))
            if n % GH == 2 and n >= GH + 2:
                jobs.append(("R", (n - 6) // GH))
            if 0 <= n - (GB * GH + 3) < QT:
                jobs.insert(0, ("x1", n - (GB * GH + 3)))
            STEP_JOBS[n] = jobs
        PMJOBS = OPEN_JOBS[GH - 1] + OPEN_JOBS[LAG - 1] + [j for n in range(STEPS) for j in STEP_JOBS[n]]
        PM_AT = {j: i for i, j in enumerate(PMJOBS)}

        POST = [("x1", t) for t in range(QT, NT)]
        for b in range(B):
            POST += [("xT", b * QT + t) for t in range(QT)] + [("logits", b), ("ohT", b)]
            for t in range(b * QT, (b + 1) * QT):
                POST += [("xmA", t), ("xmB", t)]
        POST_AT = {j: i for i, j in enumerate(POST)}

        def post_act_before(i):
            return sum(k in ("xT", "ohT", "xmA", "xmB") for k, _ in POST[:i])

        def post_dve_before(i):
            return sum(k in ("x1", "logits", "xmA", "xmB") for k, _ in POST[:i])

        def ybank(t):
            return ps[:, 3 + t // 2, t % 2 * D:(t % 2 + 1) * D]

        T_COL = {0: 0, 1: 512, 3: 896, 2: 1024}
        T_LEN = {kt: (QT - kt) * P for kt in range(QT)}
        S_COL = {3: 0, 2: 512, 0: 896, 1: 1024}
        S_LEN = {qt: (qt + 1) * P for qt in range(QT)}

        block = ctx.enter_context(nc.Block())

        @block.sync
        def _(sp):
            for b in range(B):
                sp.dma_start(xs[:, b * QT:(b + 1) * QT, :],
                             x[b].rearrange("(t p) d -> p t d", p=P)).then_inc(ld_x[b], 16)
                if b == 0:
                    sp.dma_start(wqkv[:, 0, :, :], wqT.rearrange("(k p) n -> p k n", p=P)).then_inc(ld_wq, 16)
                sp.dma_start(ctxT_s[:, :, b, :], ctxT[b, :, 0:SQ].rearrange("(k p) s -> p k s", p=P)
                             ).then_inc(ld_ctx[b], 16)
                if b == 0:
                    sp.dma_start(wqkv[:, 1, :, :], wkT.rearrange("(k p) n -> p k n", p=P)).then_inc(ld_wk, 16)
                    sp.dma_start(wqkv[:, 2, :, :], wvT.rearrange("(k p) n -> p k n", p=P)).then_inc(ld_wv, 16)

            def stack(u):
                for j in range(2):
                    s = 2 * u + j
                    sp.wait_ge(low_done, s + 1)
                    sp.dma_start(scr[s], split[:, s % 2, :, :]).then_inc(scr_done[s % 2], 16)
                    if u >= AUG and j == 0:
                        sp.wait_ge(t_fill, 2 * HU * (u - AUG + 1))
                    sp.wait_ge(scr_done[s % 2], 16 * (s // 2 + 1))
                    for r, part in enumerate(PARTS_K if j else PARTS_Q):
                        sp.dma_start(aug[r * HD:(r + 1) * HD, u % AUG, j, :, :],
                                     scr[s, :, part, :].rearrange("(h d) t -> d h t", d=HD)
                                     ).then_inc(aug_done[u % AUG], 16)

            def maxima(g):
                u, h0 = g * GH // HU, g * GH % HU
                sp.wait_ge(pm_free, PM_AT[("mT", g)] + 1)
                for part in range(2):
                    sp.dma_start(aug[KROWS + part:KROWS + part + 1, u % AUG, 0, h0:h0 + GH, :],
                                 mrow[part * GH:(part + 1) * GH, g % 2, :]).then_inc(mdma_done[g % 2], 16)

            def load_w1(c):
                if c >= 2:
                    sp.wait_ge(w1l_done, c - 1)
                for e in range(E):
                    sp.dma_start(w1f[:, c % 2, e, :, :], w1[e, :, c * P:(c + 1) * P].rearrange(
                        "(k p) i -> p k i", p=P)).then_inc(ld_w1[c % 2], 16)

            for u in range(AUG):
                stack(u)
                if u == 1:
                    sp.wait_ge(zeroed, 5)
                    for r in range(GH):
                        sp.dma_start(wo_att[32 * r:32 * r + HD, :, :], woT.rearrange(
                            "(g r d) n -> r d g n", r=GH, d=HD)[r]).then_inc(ld_woT, 16)
                    sp.dma_start(wo_s[:], wo.rearrange("(c p) n -> p c n", p=P)).then_inc(ld_wo, 16)
            maxima(0)
            maxima(1)
            sp.wait_ge(pre_act, NPRE)
            load_w1(0)
            load_w1(1)
            maxima(2)
            stack(AUG)
            for g in range(3, NG):
                maxima(g)
            for c in range(2, IC):
                load_w1(c)

            for t in range(NT):
                b = t // QT
                sp.wait_ge(z_done, t + 1)
                sp.dma_start(out[b, (t % QT) * P:(t % QT + 1) * P, :], xn[:, t, :]).then_inc(out_done, 16)
            sp.wait_ge(out_done, 16 * NT)

        @block.gpsimd
        def _(pool):
            nc.gpsimd.memset(ones_sq[:], 1.0).then_inc(veps_done, 1)
            nc.gpsimd.memset(mask[:], 0.0).then_inc(veps_done, 1)
            nc.gpsimd.memset(mhalf[:], -0.5).then_inc(veps_done, 1)
            nc.gpsimd.memset(wo_att[:], 0.0).then_inc(zeroed, 1)
            for e in range(E):
                nc.gpsimd.memset(pri[:, e:e + 1], float(E - e)).then_inc(veps_done, 1)
            pool.wait_ge(veps_done, 7)
            nc.gpsimd.affine_select(out=ident[:], in_=ones_sq[:], compare_op=ALU.is_equal, fill=0.0, base=0,
                                    pattern=[[-1, P]], channel_multiplier=1).then_inc(zeroed, 1)
            nc.gpsimd.affine_select(out=identb[:], in_=ones_sq[:], compare_op=ALU.is_equal, fill=0.0, base=0,
                                    pattern=[[-1, P]], channel_multiplier=1).then_inc(zeroed, 1)
            nc.gpsimd.affine_select(out=mask[:, SQ - P:SQ], in_=mask[:, SQ - P:SQ], compare_op=ALU.is_ge, fill=NEG,
                                    base=0, pattern=[[-1, P]], channel_multiplier=1).then_inc(zeroed, 1)
            nc.gpsimd.affine_select(out=sel[:].rearrange("p (j r) -> p j r", r=32),
                                    in_=ones_sq[:].rearrange("p (j r) -> p j r", r=32),
                                    compare_op=ALU.is_equal, fill=0.0, base=-HD,
                                    pattern=[[-32, GH], [0, 32]], channel_multiplier=1).then_inc(zeroed, 1)
            own = 7
            pool.wait_ge(zeroed, 5)
            pool.dma_start(wr_s[:], w_router.rearrange("(k p) e -> p k e", p=P)).then_inc(ld_small, 16)
            pool.dma_start(gam[:], gamma[None, :].to_broadcast([P, D])).then_inc(ld_small, 16)
            pool.dma_start(bet[:], beta[None, :].to_broadcast([P, D])).then_inc(ld_small, 16)
            pool.dma_start(bo_s[:], bo[None, :].to_broadcast([P, D])).then_inc(ld_small, 16)
            pool.wait_ge(vzero, 4)
            pool.dma_start(b1f[0:E, :], b1).then_inc(ld_b1, 16)
            pool.dma_start(b1f[32:32 + E, :], b1).then_inc(ld_b1, 16)

            def row_scale(which, b, eps, ready):
                nonlocal own
                t = slice(b * QT, (b + 1) * QT)
                pool.wait_ge(stat_done, ready)
                nc.gpsimd.tensor_scalar(veps[:, which, t], mv[:, which, t, 1], eps, None, ALU.add).then_inc(veps_done, 1)
                own += 1
                pool.wait_ge(veps_done, own)
                nc.gpsimd.tensor_tensor(rstd[:, which, t], veps[:, which, t], mhalf[:, 0:QT], ALU.pow
                                        ).then_inc(rstd_done, 1)

            for b in range(B):
                row_scale(0, b, LN_EPS, b + 1)
            for b in range(B):
                for c in range(KC):
                    for j in range(2):
                        s = 2 * (b * KC + c) + j
                        pool.wait_ge(mid_done, s + 1)
                        nc.gpsimd.tensor_tensor(split[:, s % 2, 2, :], rest[:, s % 2, :], split[:, s % 2, 1, :],
                                                ALU.subtract).then_inc(low_done, 1)

            for n in range(NH):
                pool.wait_ge(t_free, 2 * n + 2)
                pt = pT[:, n % PR, :]
                three = pt.rearrange("p (a b) -> p a b", b=2 * P)[:, 0:5:2, 0:P]
                nc.gpsimd.affine_select(out=three, in_=three, compare_op=ALU.is_ge, fill=0.0, base=0,
                                        pattern=[[0, 3], [1, P]], channel_multiplier=-1)
                one = pt[:, T_COL[3]:T_COL[3] + P]
                nc.gpsimd.affine_select(out=one, in_=one, compare_op=ALU.is_ge, fill=0.0, base=0,
                                        pattern=[[1, P]], channel_multiplier=-1).then_inc(p_masked, 1)
                if n == GB * GH + 3 + QT:
                    row_scale(1, 0, LN_EPS, B + 1)

            row_scale(1, 1, LN_EPS, B + 2)
            for c in range(IC):
                pool.wait_ge(w1h_done, c + 1)
                nc.gpsimd.tensor_tensor(w1l[:, c % 2], w1f[:, c % 2], w1h[:, c % 2].bitcast(fp32),
                                        ALU.subtract).then_inc(w1l_done, 1)
                if c == 1:
                    pool.wait_ge(ld_small, 16 * 4)
                    for b in range(B):
                        t = slice(b * QT, (b + 1) * QT)
                        pool.wait_ge(xm_done, (b + 1) * QT)
                        nc.gpsimd.tensor_tensor(xn[:, t, :], xn[:, t, :], bo_s[:].rearrange(
                            "p (o d) -> p o d", o=1).to_broadcast([P, QT, D]), ALU.add).then_inc(xb_done, 1)
                        nc.gpsimd.tensor_tensor(xs[:, t, :], xs[:, t, :], bet[:].rearrange(
                            "p (o d) -> p o d", o=1).to_broadcast([P, QT, D]), ALU.add).then_inc(xb_done, 1)
            for b in range(B):
                row_scale(2, b, FFN_EPS, 2 * B + b + 1)

        @block.scalar
        def _(act):
            for i, (kind, k) in enumerate(PRE):
                act.wait_ge(pre_fill, i + 1)
                bank = ps[:, i % 8, :]
                if kind == "xT":
                    nc.scalar.copy(xnT[:, :, k * P:(k + 1) * P], bank[:, 0:KC * P].rearrange(
                        "p (c t) -> p c t", c=KC)).then_inc(pre_act, 1)
                elif kind == "qk":
                    if k >= 2:
                        act.wait_ge(scr_done[k % 2], 16 * (k // 2))
                    nc.scalar.activation(split[:, k % 2, 0, :], bank, ACT.Copy,
                                         scale=1.0 if k % 2 else SCALE).then_inc(pre_act, 1)
                else:
                    act.wait_ge(vzero, 4)
                    nc.scalar.copy(vaug[:, k, :, 0:HD], bank[:, 0:D].rearrange("p (h d) -> p h d", d=HD)
                                   ).then_inc(pre_act, 1)

            def take_o(g):
                act.wait_ge(pv_done, g + 1)
                if g >= 2:
                    act.wait_ge(on_done, g - 1)
                nc.scalar.copy(oT[:, g % 2, :], ps[:, PO, :]).then_inc(o_done, 1)

            for n in range(NH):
                if n >= PR:
                    act.wait_ge(pv_done, n // GH - 1)
                act.wait_ge(t_fill, 2 * n + 1)
                nc.scalar.activation(pT[:, n % PR, 0:512], ps[:, T0, :], ACT.Exp).then_inc(t_free, 1)
                act.wait_ge(t_fill, 2 * n + 2)
                nc.scalar.activation(pT[:, n % PR, 512:PCOLS], ps[:, T0 + 1:T0 + 3, :].rearrange(
                    "p a b -> p (a b)")[:, 0:PCOLS - 512], ACT.Exp).then_inc(t_free, 1)
                if n % GH == 1 and n >= GH + 1:
                    take_o((n - 5) // GH)
            take_o(NG - 1)

            def cut_w1(c):
                act.wait_ge(ld_w1[c % 2], 16 * E * (c // 2 + 1))
                if c >= 2:
                    act.wait_ge(h_fill, 2 * (c - 1))
                nc.scalar.copy(w1h[:, c % 2], w1f[:, c % 2]).then_inc(w1h_done, 1)

            for c in range(2):
                cut_w1(c)
            for i, (kind, t) in enumerate(POST):
                if kind not in ("xT", "ohT", "xmA", "xmB"):
                    continue
                act.wait_ge(post_fill, i + 1)
                bank = ps[:, i % 8, :]
                if kind == "xT":
                    nc.scalar.copy(xnT[:, :, t * P:(t + 1) * P], bank[:, 0:KC * P].rearrange(
                        "p (c t) -> p c t", c=KC)).then_inc(post_act, 1)
                elif kind == "ohT":
                    nc.scalar.copy(ohT[:, t * SQ:(t + 1) * SQ], bank[0:36, :]).then_inc(post_act, 1)
                else:
                    e0 = 0 if kind == "xmA" else 2
                    half, c0 = t // QT, (t % QT) * P
                    nc.scalar.copy(xmT[half][0][:, e0:e0 + 2, :, c0:c0 + P], bank.rearrange(
                        "p (e k t) -> p e k t", e=2, k=KC)).then_inc(post_act, 1)
            for c in range(IC):
                for half in range(2):
                    i = 2 * c + half
                    act.wait_ge(h_fill, i + 1)
                    if i >= 2:
                        act.wait_ge(y_done, i - 1)
                    nc.scalar.activation(g_ring[:, i % 2, :], ps[:, i % 3, :], ACT.Gelu).then_inc(g_done, 1)
                if 2 <= c + 2 < IC:
                    cut_w1(c + 2)

        @block.vector
        def _(dve):
            nc.vector.memset(vaug[:], 0.0).then_inc(fin, 1)
            dve.wait_ge(fin, 1)
            nc.vector.memset(vaug[:, :, :, HD:HD + 1], 1.0).then_inc(vzero, 1)
            nc.vector.memset(oh[:], 0.0).then_inc(vzero, 1)
            nc.vector.memset(aug[KROWS:KROWS_M, :, 1, :, :], 1.0).then_inc(vzero, 1)
            nc.vector.memset(b1f[:], 0.0).then_inc(vzero, 1)
            own = 1

            def row_stats(which, src, b):
                nonlocal own
                for t in range(b * QT, (b + 1) * QT):
                    nc.vector.bn_stats(stats[:, which, t, :], src(t)).then_inc(fin, 1)
                own += QT
                dve.wait_ge(fin, own)
                for t in range(b * QT, (b + 1) * QT):
                    last = nc.vector.bn_aggr(mv[:, which, t, :], stats[:, which, t, :])
                last.then_inc(stat_done, 1)

            def normalise(which, src, dst, t, signal):
                nc.vector.tensor_scalar(dst, src, mv[:, which, t, 0:1], rstd[:, which, t:t + 1],
                                        ALU.subtract, ALU.mult).then_inc(signal, 1)

            for b in range(B):
                dve.wait_ge(ld_x[b], 16)
                row_stats(0, lambda t: xs[:, t, :], b)
                dve.wait_ge(rstd_done, b + 1)
                for t in range(b * QT, (b + 1) * QT):
                    normalise(0, xs[:, t, :], xn[:, t, :], t, xn_done)
            for i, (kind, k) in enumerate(PRE):
                if kind != "qk":
                    continue
                dve.wait_ge(pre_act, i + 1)
                if k >= 2:
                    dve.wait_ge(low_done, k - 1)
                nc.vector.scalar_tensor_tensor(out=rest[:, k % 2, :], in0=ps[:, i % 8, :],
                                               scalar=1.0 if k % 2 else SCALE, in1=split[:, k % 2, 0, :],
                                               op0=ALU.mult, op1=ALU.subtract).then_inc(pre_dve, 1)
                dve.wait_ge(pre_dve, dve_jobs(i) + 1)
                nc.vector.tensor_copy(split[:, k % 2, 1, :], rest[:, k % 2, :]).then_inc(mid_done, 1)

            dve.wait_ge(zeroed, 5)

            def head_max(n):
                g, j = n // GH, n % GH
                for k, tiles in enumerate(((3,), (2, 0), (1,))):
                    dve.wait_ge(s_fill, 3 * n + k + 1)
                    for qt in tiles:
                        c = S_COL[qt]
                        scores = ps[:, S0 + c // 512, c % 512:c % 512 + S_LEN[qt]]
                        last = nc.vector.tensor_tensor_reduce(
                            out=scores, in0=scores,
                            in1=mask[:, SQ - S_LEN[qt]:SQ], scale=1.0, scalar=NEG, op0=ALU.add, op1=ALU.max,
                            accum_out=mmax[:, g % 2, qt, j:j + 1])
                    last.then_inc(s_free, 1)
                if j == GH - 1:
                    if g >= 2:
                        dve.wait_ge(pm_fill, PM_AT[("mT", g - 2)] + 1)
                    dve.wait_ge(s_free, 3 * n + 3)
                    nc.vector.tensor_scalar(mparts[:, g % 2, :, 0, :], mmax[:, g % 2, :, :], -1.0, None,
                                            ALU.mult).then_inc(mh_done, 1)
                    dve.wait_ge(mh_done, g + 1)
                    nc.vector.scalar_tensor_tensor(out=mparts[:, g % 2, :, 1, :], in0=mmax[:, g % 2, :, :],
                                                   scalar=-1.0, in1=mparts[:, g % 2, :, 0, :],
                                                   op0=ALU.mult, op1=ALU.subtract).then_inc(m_done, 1)

            def pm_job(kind, g):
                at = PM_AT[(kind, g)]
                dve.wait_ge(pm_fill, at + 1)
                if kind == "mT":
                    if g >= 2:
                        dve.wait_ge(mdma_done[g % 2], 32 * (g // 2))
                    nc.vector.tensor_copy(mrow[:, g % 2, :], ps[0:2 * GH, PM, 0:SQ // 2].bitcast(bf16)
                                          ).then_inc(pm_free, 1)
                elif kind == "R":
                    if g >= 1:
                        dve.wait_ge(on_done, g)
                    nc.vector.reciprocal(rec[:], ps[:, PM, :]).then_inc(pm_free, 1)
                    dve.wait_ge(pm_free, at + 1)
                    nc.vector.tensor_tensor(onT[:, g % GB, :], oT[:, g % 2, :], rec[:], ALU.mult
                                            ).then_inc(on_done, 1)
                else:
                    nc.vector.tensor_tensor(xs[:, g, :], xs[:, g, :], ps[:, PM, 0:D], ALU.add).then_inc(pm_free, 1)
                    if g == QT - 1:
                        dve.wait_ge(pm_free, at + 1)
                        second_norm(0)

            def second_norm(b):
                row_stats(1, lambda t: xs[:, t, :], b)
                dve.wait_ge(rstd_done, B + b + 1)
                for t in range(b * QT, (b + 1) * QT):
                    normalise(1, xs[:, t, :], xn[:, t, :], t, xn_done)

            for n in range(LAG):
                head_max(n)
                for job in OPEN_JOBS.get(n, []):
                    pm_job(*job)
            for n in range(STEPS):
                if n + LAG < NH:
                    head_max(n + LAG)
                for job in STEP_JOBS[n]:
                    pm_job(*job)

            dve.wait_ge(ld_b1, 32)
            nc.vector.tensor_copy(b1s[:], b1f[:]).then_inc(fin, 1)
            own += 1
            dve.wait_ge(fin, own)
            nc.vector.tensor_tensor(b1s[32:36, :], b1f[32:36, :], b1s[32:36, :].bitcast(fp32), ALU.subtract
                                    ).then_inc(b1_done, 1)
            for i, (kind, t) in enumerate(POST):
                bank = ps[:, i % 8, :]
                if kind == "x1":
                    dve.wait_ge(post_fill, i + 1)
                    nc.vector.tensor_tensor(xs[:, t, :], xs[:, t, :], bank[:, 0:D], ALU.add).then_inc(post_dve, 1)
                    if t % QT == QT - 1:
                        b = t // QT
                        dve.wait_ge(post_dve, post_dve_before(i) + 1)
                        second_norm(b)
                elif kind == "logits":
                    b = t
                    ts = slice(b * QT, (b + 1) * QT)
                    dve.wait_ge(post_fill, i + 1)
                    nc.vector.tensor_copy(lg[:, ts, :], bank[:, 0:QT * E].rearrange("p (t e) -> p t e", e=E)
                                          ).then_inc(post_dve, 1)
                    dve.wait_ge(post_dve, post_dve_before(i) + 1)
                    step = 5 * b
                    nc.vector.tensor_reduce(lmax[:, ts], lg[:, ts, :], mybir.AxisListType.X, ALU.max
                                            ).then_inc(oh_step, 1)
                    dve.wait_ge(oh_step, step + 1)
                    nc.vector.tensor_tensor(lg[:, ts, :], lg[:, ts, :], lmax[:, ts].rearrange(
                        "p (t o) -> p t o", o=1).to_broadcast([P, QT, E]), ALU.is_equal).then_inc(oh_step, 1)
                    dve.wait_ge(oh_step, step + 2)
                    nc.vector.tensor_tensor(lg[:, ts, :], lg[:, ts, :], pri[:].rearrange(
                        "p (o e) -> p o e", o=1).to_broadcast([P, QT, E]), ALU.mult).then_inc(oh_step, 1)
                    dve.wait_ge(oh_step, step + 3)
                    nc.vector.tensor_reduce(lmax[:, ts], lg[:, ts, :], mybir.AxisListType.X, ALU.max
                                            ).then_inc(oh_step, 1)
                    dve.wait_ge(oh_step, step + 4)
                    for c0 in (0, 32):
                        last = nc.vector.tensor_tensor(oh[:, ts, c0:c0 + E], lg[:, ts, :], lmax[:, ts].rearrange(
                            "p (t o) -> p t o", o=1).to_broadcast([P, QT, E]), ALU.is_equal)
                    last.then_inc(oh_step, 1)
                    dve.wait_ge(oh_step, step + 5)
                elif kind == "xmA":
                    if t >= 2:
                        dve.wait_ge(post_fill, POST_AT[("xmB", t - 2)] + 1)
                    for e in range(E):
                        last = nc.vector.tensor_scalar(xm_s[:, t % 2, e * D:(e + 1) * D], xn[:, t, :],
                                                       oh[:, t, e:e + 1], None, ALU.mult)
                    last.then_inc(xm_done, 1)
                if kind in ("xmA", "xmB"):
                    e0 = 0 if kind == "xmA" else 2
                    half, c0 = t // QT, (t % QT) * P
                    dve.wait_ge(post_act, post_act_before(i) + 1)
                    nc.vector.tensor_tensor(xmT[half][1][:, e0:e0 + 2, :, c0:c0 + P],
                                            bank.rearrange("p (e k t) -> p e k t", e=2, k=KC),
                                            xmT[half][0][:, e0:e0 + 2, :, c0:c0 + P].bitcast(fp32),
                                            ALU.subtract).then_inc(post_dve, 1)

            dve.wait_ge(ld_small, 16 * 4)
            for b in range(B):
                dve.wait_ge(y_done, 2 * (IC - 1) + b + 1)
                dve.wait_ge(xb_done, 2 * b + 2)
                for t in range(b * QT, (b + 1) * QT):
                    nc.vector.tensor_tensor(xn[:, t, :], ybank(t), xn[:, t, :], ALU.add).then_inc(fin, 1)
                own += QT
                dve.wait_ge(fin, own)
                row_stats(2, lambda t: xn[:, t, :], b)
                dve.wait_ge(rstd_done, 2 * B + b + 1)
                for t in range(b * QT, (b + 1) * QT):
                    normalise(2, xn[:, t, :], xn[:, t, :], t, fin)
                own += QT
                dve.wait_ge(fin, own)
                for t in range(b * QT, (b + 1) * QT):
                    nc.vector.tensor_tensor(xn[:, t, :], xn[:, t, :], gam[:], ALU.mult).then_inc(fin, 1)
                own += QT
                dve.wait_ge(fin, own)
                for t in range(b * QT, (b + 1) * QT):
                    nc.vector.tensor_tensor(xn[:, t, :], xn[:, t, :], xs[:, t, :], ALU.add).then_inc(z_done, 1)


        @block.tensor
        def _(pe):
            pe.wait_ge(zeroed, 5)
            for i, (kind, k) in enumerate(PRE):
                b = i // (NPRE // B)
                if i >= 8:
                    if PRE[i - 8][0] == "qk":
                        pe.wait_ge(pre_dve, dve_jobs(i - 8) + 1)
                    else:
                        pe.wait_ge(pre_act, i - 7)
                bank = ps[:, i % 8, :]
                if kind == "xT":
                    pe.wait_ge(xn_done, k + 1)
                    for c in range(KC):
                        last = nc.tensor.transpose(bank[:, c * P:(c + 1) * P], xn[:, k, c * P:(c + 1) * P], ident[:])
                elif kind == "qk":
                    u, j = k // 2, k % 2
                    if j == 0:
                        pe.wait_ge(ld_wq, 16)
                        pe.wait_ge(pre_act, b * (NPRE // B) + QT)
                    else:
                        pe.wait_ge(ld_wk, 16)
                        pe.wait_ge(ld_ctx[b], 16)
                    for c in range(KC):
                        src = ctxT_s[:, c, b, :] if j else xnT[:, c, b * SQ:(b + 1) * SQ]
                        last = nc.tensor.matmul(bank, wqkv[:, j, c, u % KC * P:(u % KC + 1) * P], src,
                                                start=(c == 0), stop=(c == KC - 1))
                else:
                    pe.wait_ge(ld_wv, 16)
                    for c in range(KC):
                        last = nc.tensor.matmul(bank[:, 0:D], ctxT_s[:, c, b, k % QT * P:(k % QT + 1) * P],
                                                wqkv[:, 2, c, :], start=(c == 0), stop=(c == KC - 1))
                last.then_inc(pre_fill, 1)

            pe.wait_ge(pre_act, NPRE)
            pe.wait_ge(pre_dve, 2 * NU)
            pe.wait_ge(vzero, 4)

            def scores(n):
                u, h = n // HU, n % HU
                if h == 0:
                    pe.wait_ge(aug_done[u % AUG], 16 * 2 * len(PARTS_Q) * (u // AUG + 1))
                for k, tiles in enumerate(((3,), (2, 0), (1,))):
                    if n >= 1:
                        pe.wait_ge(s_free, 3 * (n - 1) + k + 1)
                    for qt in tiles:
                        c = S_COL[qt]
                        last = nc.tensor.matmul(ps[:, S0 + c // 512, c % 512:c % 512 + S_LEN[qt]],
                                                aug[0:KROWS, u % AUG, 0, h, qt * P:(qt + 1) * P],
                                                aug[0:KROWS, u % AUG, 1, h, 0:S_LEN[qt]], start=True, stop=True)
                    last.then_inc(s_fill, 1)

            def scores_T(n):
                u, h = n // HU, n % HU
                if n % GH == 0:
                    g = n // GH
                    pe.wait_ge(mdma_done[g % 2], 32 * (g // 2 + 1))
                for k, tiles in enumerate(((0,), (1, 3), (2,))):
                    if n >= 1 and k < 2:
                        pe.wait_ge(t_free, 2 * (n - 1) + k + 1)
                    for kt in tiles:
                        c = T_COL[kt]
                        last = nc.tensor.matmul(ps[:, T0 + c // 512, c % 512:c % 512 + T_LEN[kt]],
                                                aug[0:KROWS_M, u % AUG, 1, h, kt * P:(kt + 1) * P],
                                                aug[0:KROWS_M, u % AUG, 0, h, kt * P:SQ], start=True, stop=True)
                    if k != 1:
                        last.then_inc(t_fill, 1)

            def weigh(g):
                pe.wait_ge(p_masked, GH * (g + 1))
                if g >= 1:
                    pe.wait_ge(o_done, g)
                b = g // GB
                for kt in range(QT):
                    for j in range(GH):
                        n = g * GH + j
                        last = nc.tensor.matmul(ps[32 * j:32 * j + 32, PO, kt * P:SQ],
                                                vaug[:, b * QT + kt, n % H, :],
                                                pT[:, n % PR, T_COL[kt]:T_COL[kt] + T_LEN[kt]],
                                                start=(kt == 0), stop=(kt == QT - 1), skip_group_check=True)
                last.then_inc(pv_done, 1)

            def times_wo(dst, t):
                for g in range(GB):
                    last = nc.tensor.matmul(dst, onT[:, g, t % QT * P:(t % QT + 1) * P], wo_att[:, g, :],
                                            start=(g == 0), stop=(g == GB - 1))
                return last

            def pm_job(kind, g):
                at = PM_AT[(kind, g)]
                if at >= 1:
                    pe.wait_ge(pm_free, at)
                if kind == "mT":
                    pe.wait_ge(m_done, g + 1)
                    for qt in range(QT):
                        last = nc.tensor.transpose(ps[0:2 * GH, PM, qt * P // 2:(qt + 1) * P // 2].bitcast(bf16),
                                                   mparts[:, g % 2, qt, :, :].rearrange("p a b -> p (a b)"),
                                                   identb[:])
                elif kind == "R":
                    pe.wait_ge(o_done, g + 1)
                    last = nc.tensor.matmul(ps[:, PM, :], sel[:], oT[:, g % 2, :], start=True, stop=True)
                else:
                    if g == 0:
                        pe.wait_ge(ld_woT, 16 * GH)
                        pe.wait_ge(on_done, GB)
                    last = times_wo(ps[:, PM, 0:D], g)
                last.then_inc(pm_fill, 1)

            for n in range(LAG):
                scores(n)
                for job in OPEN_JOBS.get(n, []):
                    pm_job(*job)
            for n in range(STEPS):
                if n + LAG < NH:
                    scores(n + LAG)
                if n < NH:
                    scores_T(n)
                if n % GH == 1 and n >= GH + 1:
                    weigh((n - GH - 1) // GH)
                for job in STEP_JOBS[n]:
                    pm_job(*job)

            pe.wait_ge(s_free, 3 * NH)
            pe.wait_ge(t_free, 2 * NH)
            pe.wait_ge(pm_free, len(PMJOBS))
            for i, (kind, t) in enumerate(POST):
                if i >= 8:
                    if POST[i - 8][0] in ("xT", "ohT"):
                        pe.wait_ge(post_act, post_act_before(i - 8) + 1)
                    else:
                        pe.wait_ge(post_dve, post_dve_before(i - 8) + 1)
                bank = ps[:, i % 8, :]
                if kind == "x1":
                    pe.wait_ge(on_done, NG)
                    last = times_wo(bank[:, 0:D], t)
                elif kind == "xT":
                    pe.wait_ge(xn_done, NT + t + 1)
                    for c in range(KC):
                        last = nc.tensor.transpose(bank[:, c * P:(c + 1) * P], xn[:, t, c * P:(c + 1) * P], ident[:])
                elif kind == "logits":
                    pe.wait_ge(ld_small, 16 * 4)
                    pe.wait_ge(post_act, post_act_before(POST_AT[("xT", t * QT + QT - 1)]) + 1)
                    for j in range(QT):
                        for c in range(KC):
                            tt = t * QT + j
                            last = nc.tensor.matmul(bank[:, j * E:(j + 1) * E], xnT[:, c, tt * P:(tt + 1) * P],
                                                    wr_s[:, c, :], start=(c == 0), stop=(c == KC - 1))
                elif kind == "ohT":
                    pe.wait_ge(oh_step, 5 * (t + 1))
                    for j in range(QT):
                        last = nc.tensor.transpose(bank[0:36, j * P:(j + 1) * P], oh[:, t * QT + j, :], ident[:])
                else:
                    if kind == "xmA":
                        pe.wait_ge(xm_done, t + 1)
                    e0 = 0 if kind == "xmA" else 2
                    for j in range(2 * KC):
                        c0 = e0 * D + j * P
                        last = nc.tensor.transpose(bank[:, j * P:(j + 1) * P], xm_s[:, t % 2, c0:c0 + P], ident[:])
                last.then_inc(post_fill, 1)

            pe.wait_ge(post_act, post_act_before(len(POST)))
            pe.wait_ge(post_dve, post_dve_before(len(POST)))
            pe.wait_ge(b1_done, 1)
            pe.wait_ge(ld_wo, 16)

            def hidden(i):
                c, half = i // 2, i % 2
                if half == 0:
                    pe.wait_ge(w1l_done, c + 1)
                if i >= 3:
                    pe.wait_ge(g_done, i - 2)
                bank = ps[:, i % 3, :]
                nc.tensor.matmul(bank, b1s[:, c * P:(c + 1) * P], ohT[:, half * SQ:(half + 1) * SQ],
                                 start=True, stop=False)
                for e in range(E):
                    for k in range(KC):
                        for w, part in ((w1h, 0), (w1l, 0), (w1h, 1)):
                            last = nc.tensor.matmul(bank, w[:, c % 2, e, k, :], xmT[half][part][:, e, k, :],
                                                    start=False, stop=(w is w1h and part == 1 and e == E - 1
                                                                       and k == KC - 1))
                last.then_inc(h_fill, 1)

            def share(i):
                c, half = i // 2, i % 2
                pe.wait_ge(g_done, i + 1)
                for j in range(QT):
                    last = nc.tensor.matmul(ybank(half * QT + j), g_ring[:, i % 2, j * P:(j + 1) * P],
                                            wo_s[:, c, :], start=(c == 0 and j % 2 == 0), stop=(c == IC - 1),
                                            skip_group_check=True)
                last.then_inc(y_done, 1)

            hidden(0)
            for i in range(1, 2 * IC):
                hidden(i)
                share(i - 1)
            share(2 * IC - 1)


def kernel(x, ctx_1024, L0_xattn_Wq, L0_xattn_Wk, L0_xattn_Wv, L0_xattn_Wo, L0_ffn_W_router, L0_ffn_W1, L0_ffn_b1,
           L0_ffn_Wo, L0_ffn_bo, L0_ffn_ln_gamma, L0_ffn_ln_beta):
    import numpy as np
    import concourse.bacc as bacc
    from concourse import mybir
    from concourse.bass_utils import run_bass_kernel_spmd

    laid = {
        "x": x, "ctxT": np.transpose(ctx_1024, (0, 2, 1)),
        "wqT": np.transpose(L0_xattn_Wq), "wkT": np.transpose(L0_xattn_Wk), "wvT": np.transpose(L0_xattn_Wv),
        "woT": np.transpose(L0_xattn_Wo), "w_router": L0_ffn_W_router, "w1": L0_ffn_W1, "b1": L0_ffn_b1,
        "wo": L0_ffn_Wo, "bo": L0_ffn_bo, "gamma": L0_ffn_ln_gamma, "beta": L0_ffn_ln_beta,
    }
    nc = bacc.Bacc("TRN2", target_bir_lowering=False, num_devices=1)
    arrays, aps = {}, []
    for name, a in laid.items():
        a = np.ascontiguousarray(a)
        arrays[f"in_{name}"] = a
        aps.append(nc.dram_tensor(f"in_{name}", a.shape, mybir.dt.from_np(a.dtype), kind="ExternalInput").ap())
    out = nc.dram_tensor("out_x", arrays["in_x"].shape, mybir.dt.float32, kind="ExternalOutput").ap()
    cross_attention_moe_ffn(nc, *aps, out)
    r = run_bass_kernel_spmd(nc, [arrays], core_ids=[0])
    return r.results[0]["out_x"]
```

```python
import concourse.bass as bass
from concourse import mybir
from contextlib import ExitStack


def cross_attention_moe_ffn(nc: bass.Bass, x, ctxT, wqT, wkT, wvT, woT, w_router, w1, b1, wo, bo, gamma, beta, out):
    fp32, bf16, f32r = mybir.dt.float32, mybir.dt.bfloat16, mybir.dt.float32r
    ALU, ACT = mybir.AluOpType, mybir.ActivationFunctionType

    P = 128
    B, SQ, D = x.shape
    HD = 16
    H = D // HD
    SCALE = HD ** -0.5
    KC = D // P
    QT = SQ // P
    NT = B * QT
    HU = P // HD
    NU = B * KC
    GH = 4
    NG = B * H // GH
    GB = NG // B
    NH = B * H
    BK = 32
    E, _, I = w1.shape
    IC = I // P
    LN_EPS, FFN_EPS = 1e-5, 1e-12
    RUNS_Q = ((0, 1), (0, 1, 2), (0,))
    RUNS_K = ((0, 1, 2), (0,), (0, 1))
    KROWS = HD * sum(len(r) for r in RUNS_Q)
    KROWS_M = KROWS + 2
    PCOLS = P * QT * (QT + 1) // 2
    VW = HD + 1
    OR = 3 * BK
    NEG = -1.0e30
    LAG = 7
    MT_PLACE = 1
    AHEAD = 3
    HALF0_REST = [[], [("logits", 0)], [], [("ohT", 0)], [], [("mk", e) for e in range(E)]]
    HID_AT = (28, 29, 30, 31)
    DVE_M0, POOL_M0 = 26, 29
    SLOTS = 4
    PR = 6
    RW = 3

    ctx = ExitStack()
    with ctx:
        SBUF_BASE = 16512
        place = {"next": SBUF_BASE}

        def width(shape, dt):
            n = mybir.dt.size(dt)
            for d in shape[1:]:
                n *= d
            return -(-n // 32) * 32

        def sb(name, shape, dt=fp32):
            at = place["next"]
            place["next"] = at + width(shape, dt)
            place[name] = at
            return nc.alloc_sbuf_tensor_at(name, shape, dt, offset=at)

        def over(name, shape, dt, first, skip=0):
            return nc.alloc_sbuf_tensor_at(name, shape, dt, offset=place[first] + skip)

        def sem(name):
            return ctx.enter_context(nc.semaphore(name))

        xs = sb("xs", [P, NT, D])
        xn = sb("xn", [P, NT, D])
        xnT = sb("xnT", [P, KC, B * SQ])
        ctxT_s = sb("ctxT_s", [P, KC, B, SQ])
        w1f = over("w1f", [P, E, KC, P], fp32, "ctxT_s")
        b1f = over("b1f", [OR, I], fp32, "ctxT_s", 4 * E * KC * P)
        wqkv = sb("wqkv", [P, 3, KC, D])
        mk = over("mk", [P, E, SQ], bf16, "wqkv")
        wo_att = sb("wo_att", [P, GB // 2, D])
        vaug = sb("vaug", [P, NT, H * VW + BK - VW])
        aug = sb("aug", [P, SLOTS, 2, GH, SQ], bf16)
        pT = sb("pT", [P, PR, PCOLS])
        XB = E * KC * SQ * 4
        xmT0h, xmT0l = sb("xmT0h", [P, E, KC, SQ], f32r), sb("xmT0l", [P, E, KC, SQ], f32r)
        xmT1h, xmT1l = over("xmT1h", [P, E, KC, SQ], f32r, "aug"), over("xmT1l", [P, E, KC, SQ], f32r, "aug", XB)
        xmT = ((xmT0h, xmT0l), (xmT1h, xmT1l))
        split = sb("split", [P, 2, 3, SQ], bf16)
        rest = sb("rest", [P, 2, SQ])
        ohT = over("ohT", [OR, B * SQ], f32r, "split")
        sel = over("sel", [OR, E, P], f32r, "split", 4 * B * SQ)
        b1s = over("b1s", [OR, I], f32r, "rest")
        oq = sb("oq", [P, 2, SQ // BK, BK])
        onT = sb("onT", [P, GB // 2, SQ])
        xh, xl = sb("xh", [P, KC, SQ], f32r), sb("xl", [P, KC, SQ], f32r)
        WB = E * KC * P * 4
        w1h = [sb("w1h0", [P, E, KC, P], f32r), sb("w1h1", [P, E, KC, P], f32r),
               over("w1h2", [P, E, KC, P], f32r, "pT")]
        w1l = [sb("w1l0", [P, E, KC, P], f32r), sb("w1l1", [P, E, KC, P], f32r),
               over("w1l2", [P, E, KC, P], f32r, "pT", WB)]
        GW = 4 * 2 * SQ
        g_ring = sb("g_ring", [P, 2, SQ])
        g_h = over("g_h", [P, 2, SQ], f32r, "pT", 2 * WB)
        g_l = over("g_l", [P, 2, SQ], f32r, "pT", 2 * WB + GW)
        wo_h = over("wo_h", [P, IC, D], f32r, "pT", 2 * WB + 2 * GW)
        wo_l = over("wo_l", [P, IC, D], f32r, "vaug")
        wo_s = sb("wo_s", [P, IC, D])
        wr_s = sb("wr_s", [P, KC, E])
        gam = sb("gam", [P, D])
        bet = sb("bet", [P, D])
        bo_s = sb("bo_s", [P, D])
        mask = sb("mask", [P, SQ], bf16)
        ones_sq = over("ones_sq", [P, P], fp32, "xl")
        ident = sb("ident", [P, P])
        identb = sb("identb", [P, P], bf16)
        ones_row = over("ones_row", [2, SQ], bf16, "xl", 4 * P)
        picks = over("picks", [OR, E, P], fp32, "xh")
        mhalf = sb("mhalf", [P, 1])
        mmax = sb("mmax", [P, 2, QT, GH])
        mparts = sb("mparts", [P, 2, QT, 2, GH], bf16)
        mrow = sb("mrow", [2 * GH, 2, SQ], bf16)
        rsum = sb("rsum", [P, SQ // BK])
        stats = sb("stats", [P, 3, NT, 6])
        mv = sb("mv", [P, 3, NT, 2])
        veps = sb("veps", [P, 3, NT])
        rstd = sb("rstd", [P, 3, NT])
        lg = sb("lg", [P, NT, E])
        lmax = sb("lmax", [P, NT])
        pri = sb("pri", [P, E])
        oh = sb("oh", [P, QT, OR])

        ps = ctx.enter_context(nc.psum_tensor("ps", [P, 8, 512], fp32))
        S0, T0, PO, PM = 0, 3, 6, 7
        PRE_RING = (3, 4, 5, 6)
        H_RING = (0, 1, 2)

        def h_bank(i, k=0):
            return H_RING[(i + k) % 3]

        def ybank(t):
            return ps[:, 3 + t // 2, t % 2 * D:(t % 2 + 1) * D]

        ld_x = [sem(f"ld_x{b}") for b in range(B)]
        ld_ctx = [sem(f"ld_ctx{b}") for b in range(B)]
        ld_wq, ld_wk, ld_wv = sem("ld_wq"), sem("ld_wk"), sem("ld_wv")
        ld_small, ld_woT, ld_b1, ld_wo, ld_w1 = (sem(n) for n in ("ld_small", "ld_woT", "ld_b1", "ld_wo", "ld_w1"))
        ld_ones = sem("ld_ones")
        consts = sem("consts")
        pool_own = sem("pool_own")
        dve_own = sem("dve_own")
        stat_done = sem("stat_done")
        rstd_done = sem("rstd_done")
        xn_done = sem("xn_done")
        pre_fill = sem("pre_fill")
        pre_act = sem("pre_act")
        rest_done = sem("rest_done")
        mid_done = sem("mid_done")
        low_done = sem("low_done")
        scr_done = [sem("scr_done0"), sem("scr_done1")]
        aug_done = [sem(f"aug_done{s}") for s in range(SLOTS)]
        s_fill = sem("s_fill")
        s_free = sem("s_free")
        m_high = sem("m_high")
        m_done = sem("m_done")
        mdma_done = [sem("mdma_done0"), sem("mdma_done1")]
        t_fill = sem("t_fill")
        t_free = sem("t_free")
        p_masked = sem("p_masked")
        pv_done = sem("pv_done")
        o_taken = sem("o_taken")
        on_done = sem("on_done")
        misc_fill = sem("misc_fill")
        misc_act = sem("misc_act")
        misc_dve = sem("misc_dve")
        oh_step = sem("oh_step")
        picks_done = sem("picks_done")
        sel_done = sem("sel_done")
        x_parts = sem("x_parts")
        xm_dve = sem("xm_dve")
        xm_pool = sem("xm_pool")
        wo_high = sem("wo_high")
        wo_low = sem("wo_low")
        gh_done = sem("gh_done")
        gl_done = sem("gl_done")
        b1_zero = sem("b1_zero")
        b1_done = sem("b1_done")
        w1h_done = sem("w1h_done")
        w1l_done = sem("w1l_done")
        h_fill = sem("h_fill")
        g_done = sem("g_done")
        y_done = sem("y_done")
        xb_done = sem("xb_done")
        z_done = sem("z_done")
        out_done = sem("out_done")

        scr = nc.dram_tensor("parts_scratch", (2 * NU, HU, 3, HD, SQ), bf16, kind="Internal").ap()

        PRE_A = [("k", 0)] + [("xT", t) for t in range(QT)] + [("q", 0), ("k", 1), ("q", 1)]
        OPEN = {0: [("v", 0), ("v", 1), ("v", 2), ("v", 3)],
                1: [("xT", 4), ("xT", 5), ("xT", 6), ("xT", 7)], 2: [("k", 2)], 3: [("q", 2)], 4: [("k", 3)],
                5: [("q", 3)], 6: [("v", 4), ("v", 5), ("v", 6), ("v", 7)]}
        PRE = PRE_A + [j for n in range(LAG) for j in OPEN[n]]
        PRE_AT = {j: i for i, j in enumerate(PRE)}
        CUTS = [j for j in PRE if j[0] in "kq"]
        CUT_AT = {j: i for i, j in enumerate(CUTS)}

        STEPS = NH + 2
        OPEN_MISC = {n: [] for n in range(LAG)}
        STEP_MISC = {(n, w): [] for n in range(STEPS) for w in range(2)}
        for g in range(NG):
            n = GH * g + GH - LAG
            if n >= 0:
                STEP_MISC[n, MT_PLACE].append(("mT", g))
            else:
                OPEN_MISC[n + LAG].append(("mT", g))
        at = 2 * (GB * GH + 3)
        for i, jobs in enumerate([[("x1", t)] for t in range(QT)] + [[("xT", t)] for t in range(QT)] + HALF0_REST):
            STEP_MISC[(at + i) // 2, (at + i) % 2] += jobs
        LATE_A = [("x1", t) for t in range(QT, NT)]
        LATE_B = [("xT", t) for t in range(QT, NT)] + [("logits", 1)]
        LATE_C = [("ohT", 1)]
        LATE_D = [("mk", i) for i in range(E, 2 * E)]
        MISC = [j for n in range(LAG) for j in OPEN_MISC[n]] + [
            j for n in range(STEPS) for w in range(2) for j in STEP_MISC[n, w]]
        MISC_BANK = [{1: 0, 2: 1, 3: 2}.get(k, PM) if kind == "mk" else PM for kind, k in MISC]
        LATE = LATE_A + LATE_B + LATE_C + LATE_D
        MISC_BANK += [(PM, 5, PO)[i % 3] for i in range(len(LATE))]
        MISC += LATE
        MISC_AT = {j: i for i, j in enumerate(MISC)}
        BY_ACT, BY_DVE = ("mT", "xT", "ohT", "mk"), ("x1", "logits")

        def act_no(job):
            return sum(k in BY_ACT for k, _ in MISC[:MISC_AT[job] + 1])

        def dve_no(job):
            return sum(k in BY_DVE for k, _ in MISC[:MISC_AT[job] + 1])

        XM_DVE = {0: [(0, 0), (0, 1), (1, 0), (1, 1), (2, 0), (2, 1)], 1: [(0, 0), (0, 1), (1, 0), (2, 0), (2, 1)]}
        XM_POOL = {0: [(3, 0), (3, 1)], 1: [(1, 1), (3, 0), (3, 1)]}

        def spread_mask(e):
            return mk[:, e, :].rearrange("p (o t) -> p o t", o=1).to_broadcast([P, KC, SQ])

        def bank_of(job):
            return ps[:, MISC_BANK[MISC_AT[job]], :]

        MIDDLE = [(c, h) for c in range(RW, IC - AHEAD) for h in range(2)]
        UNITS = [(c, h) for h in range(2) for c in range(RW)] + MIDDLE + [
            (c, h) for h in range(2) for c in range(IC - AHEAD, IC)]
        UNIT_AT = {u: i for i, u in enumerate(UNITS)}
        END0 = UNIT_AT[(IC - 1, 0)]

        T_COL = {0: 0, 1: 512, 3: 896, 2: 1024}
        T_LEN = {kt: (QT - kt) * P for kt in range(QT)}
        S_COL = {3: 0, 2: 512, 0: 896, 1: 1024}
        S_LEN = {qt: (qt + 1) * P for qt in range(QT)}

        block = ctx.enter_context(nc.Block())

        @block.sync
        def _(sp):
            sp.dma_start(wqkv[:, 1, :, :], wkT.rearrange("(k p) n -> p k n", p=P)).then_inc(ld_wk, 16)
            for b in range(B):
                if b == 0:
                    sp.dma_start(ctxT_s[:, :, b, :], ctxT[b, :, 0:SQ].rearrange("(k p) s -> p k s", p=P)
                                 ).then_inc(ld_ctx[b], 16)
                sp.dma_start(xs[:, b * QT:(b + 1) * QT, :],
                             x[b].rearrange("(t p) d -> p t d", p=P)).then_inc(ld_x[b], 16)
                if b == 0:
                    sp.dma_start(wqkv[:, 0, :, :], wqT.rearrange("(k p) n -> p k n", p=P)).then_inc(ld_wq, 16)
                    sp.dma_start(wqkv[:, 2, :, :], wvT.rearrange("(k p) n -> p k n", p=P)).then_inc(ld_wv, 16)
            sp.dma_start(ctxT_s[:, :, 1, :], ctxT[1, :, 0:SQ].rearrange("(k p) s -> p k s", p=P)
                         ).then_inc(ld_ctx[1], 16)

            def parts_out(kind, u):
                s = CUT_AT[(kind, u)]
                for part, made in enumerate((pre_act, mid_done, low_done)):
                    sp.wait_ge(made, s + 1 if part else PRE_AT[(kind, u)] + 1)
                    sp.dma_start(scr[s, :, part, :, :], split[:, s % 2, part, :]).then_inc(scr_done[s % 2], 16)

            def stack(kind, g):
                u, h0 = g * GH // HU, g * GH % HU
                s, j = CUT_AT[(kind, u)], "qk".index(kind)
                sp.wait_ge(scr_done[s % 2], 16 * 3 * (s // 2 + 1))
                if g >= SLOTS:
                    sp.wait_ge(t_fill, 2 * GH * (g - SLOTS + 1))
                r0 = 0
                for run in (RUNS_Q, RUNS_K)[j]:
                    sp.dma_start(aug[r0:r0 + len(run) * HD, g % SLOTS, j, :, :],
                                 scr[s, h0:h0 + GH, 0:len(run), :, :].rearrange("h a d t -> (a d) h t")
                                 ).then_inc(aug_done[g % SLOTS], 16)
                    r0 += len(run) * HD

            def load_w1(c):
                if c >= 1:
                    sp.wait_ge(w1l_done, c)
                for e in range(E):
                    sp.dma_start(w1f[:, e, :, :], w1[e, :, c * P:(c + 1) * P].rearrange(
                        "(k p) i -> p k i", p=P)).then_inc(ld_w1, 16)

            parts_out("k", 0)
            stack("k", 0)
            parts_out("q", 0)
            stack("q", 0)
            parts_out("k", 1)
            stack("k", 1)
            parts_out("q", 1)
            stack("q", 1)
            parts_out("k", 2)
            stack("k", 2)
            stack("q", 2)
            parts_out("q", 2)
            parts_out("k", 3)
            stack("k", 3)
            stack("q", 3)
            parts_out("q", 3)
            for r in range(GH):
                for a in range(2):
                    sp.dma_start(wo_att[BK * r + HD * a:BK * r + HD * (a + 1), :, :], woT.rearrange(
                        "(g a r d) n -> r a d g n", a=2, r=GH, d=HD)[r, a]).then_inc(ld_woT, 16)
            sp.dma_start(wo_s[:], wo.rearrange("(c p) n -> p c n", p=P)).then_inc(ld_wo, 16)
            for g in range(SLOTS, NG):
                stack("k", g)
                stack("q", g)
                if g == SLOTS:
                    sp.wait_ge(pre_act, len(PRE))
                    load_w1(0)
                    sp.wait_ge(b1_zero, 1)
                    for r in (0, BK):
                        sp.dma_start(b1f[r:r + E, :], b1).then_inc(ld_b1, 16)
            load_w1(1)
            for c in range(2, IC):
                load_w1(c)

            for t in range(NT):
                sp.wait_ge(z_done, t + 1)
                sp.dma_start(out[t // QT, t % QT * P:(t % QT + 1) * P, :], xn[:, t, :]).then_inc(out_done, 16)
            sp.wait_ge(out_done, 16 * NT)

        @block.gpsimd
        def _(pool):
            nc.gpsimd.memset(mhalf[:], -0.5).then_inc(consts, 1)
            nc.gpsimd.memset(ones_sq[:], 1.0).then_inc(consts, 1)
            nc.gpsimd.memset(ones_row[:], 1.0).then_inc(consts, 1)
            pool.wait_ge(consts, 3)
            nc.gpsimd.affine_select(out=ident[:], in_=ones_sq[:], compare_op=ALU.is_equal, fill=0.0, base=0,
                                    pattern=[[-1, P]], channel_multiplier=1).then_inc(consts, 1)
            own = 0
            n_rows = 0

            def row_scale(which, t, eps):
                nonlocal own, n_rows
                n_rows += 1
                pool.wait_ge(stat_done, n_rows)
                nc.gpsimd.tensor_scalar(veps[:, which, t:t + 1], mv[:, which, t, 1:2], eps, None, ALU.add
                                        ).then_inc(pool_own, 1)
                own += 1
                pool.wait_ge(pool_own, own)
                nc.gpsimd.tensor_tensor(rstd[:, which, t:t + 1], veps[:, which, t:t + 1], mhalf[:], ALU.pow
                                        ).then_inc(rstd_done, 1)

            def low_part(job):
                s = CUT_AT[job]
                pool.wait_ge(mid_done, s + 1)
                nc.gpsimd.tensor_tensor(split[:, s % 2, 2, :], rest[:, s % 2, :], split[:, s % 2, 1, :],
                                        ALU.subtract).then_inc(low_done, 1)

            for t in range(QT):
                row_scale(0, t, LN_EPS)
            nc.gpsimd.memset(mask[:], 0.0).then_inc(pool_own, 1)
            own += 1
            pool.wait_ge(pool_own, own)
            nc.gpsimd.affine_select(out=mask[:, SQ - P:SQ], in_=mask[:, SQ - P:SQ], compare_op=ALU.is_ge, fill=NEG,
                                    base=0, pattern=[[-1, P]], channel_multiplier=1).then_inc(consts, 1)
            nc.gpsimd.affine_select(out=identb[:], in_=ones_sq[:], compare_op=ALU.is_equal, fill=0.0, base=0,
                                    pattern=[[-1, P]], channel_multiplier=1).then_inc(consts, 1)
            low_part(("k", 0))
            low_part(("q", 0))
            nc.gpsimd.memset(vaug[:, :, H * VW:], 0.0).then_inc(consts, 1)
            nc.gpsimd.memset(vaug[:, :, 0:H * VW].rearrange("p t (h v) -> p t h v", v=VW)[:, :, :, HD:VW], 1.0
                             ).then_inc(consts, 1)
            low_part(("k", 1))
            low_part(("q", 1))
            for t in range(QT, NT):
                row_scale(0, t, LN_EPS)
            for e in range(E):
                nc.gpsimd.memset(pri[:, e:e + 1], float(E - e)).then_inc(consts, 1)
            nc.gpsimd.memset(oh[:], 0.0).then_inc(consts, 1)
            nc.gpsimd.memset(picks[:], 1.0).then_inc(pool_own, 1)
            own += 1
            pool.wait_ge(pool_own, own)
            nc.gpsimd.affine_select(out=picks[:], in_=picks[:], compare_op=ALU.is_equal, fill=0.0, base=0,
                                    pattern=[[-1, E], [0, P]], channel_multiplier=1).then_inc(picks_done, 1)
            pool.dma_start(wr_s[:], w_router.rearrange("(k p) e -> p k e", p=P)).then_inc(ld_small, 16)
            pool.dma_start(gam[:], gamma[None, :].to_broadcast([P, D])).then_inc(ld_small, 16)
            pool.dma_start(bet[:], beta[None, :].to_broadcast([P, D])).then_inc(ld_small, 16)
            pool.dma_start(bo_s[:], bo[None, :].to_broadcast([P, D])).then_inc(ld_small, 16)
            for job in CUTS[4:]:
                low_part(job)
            pool.wait_ge(pre_act, len(PRE))
            nc.gpsimd.memset(b1f[:], 0.0).then_inc(b1_zero, 1)

            def causal(n):
                pool.wait_ge(t_free, 2 * n + 2)
                pt = pT[:, n % PR, :]
                three = pt.rearrange("p (a b) -> p a b", b=2 * P)[:, 0:5:2, 0:P]
                nc.gpsimd.affine_select(out=three, in_=three, compare_op=ALU.is_ge, fill=0.0, base=0,
                                        pattern=[[0, 3], [1, P]], channel_multiplier=-1)
                one = pt[:, T_COL[3]:T_COL[3] + P]
                nc.gpsimd.affine_select(out=one, in_=one, compare_op=ALU.is_ge, fill=0.0, base=0,
                                        pattern=[[1, P]], channel_multiplier=-1).then_inc(p_masked, 1)

            def masked(b):
                pool.wait_ge(x_parts, 2 * (b + 1))
                for e, part in XM_POOL[b]:
                    pool.wait_ge(misc_act, act_no(("mk", E * b + e)))
                    nc.gpsimd.tensor_tensor(xmT[b][part][:, e, :, :], (xh, xl)[part][:].bitcast(fp32), spread_mask(e),
                                            ALU.mult).then_inc(xm_pool, 1)

            def cut_low(c):
                pool.wait_ge(w1h_done, c + 1)
                nc.gpsimd.tensor_tensor(w1l[c % RW][:], w1f[:], w1h[c % RW][:].bitcast(fp32),
                                        ALU.subtract).then_inc(w1l_done, 1)

            def addends(b):
                t = slice(b * QT, (b + 1) * QT)
                for dst, src in ((xn, bo_s), (xs, bet)):
                    nc.gpsimd.tensor_tensor(dst[:, t, :], dst[:, t, :], src[:].rearrange(
                        "p (o d) -> p o d", o=1).to_broadcast([P, QT, D]), ALU.add).then_inc(xb_done, 1)

            for n in range(NH):
                for w in range(2):
                    if w == 1:
                        causal(n)
                    for kind, t in STEP_MISC[n, w]:
                        if kind == "x1":
                            row_scale(1, t, LN_EPS)
                if n == 20:
                    cut_low(0)
                if n == 27:
                    cut_low(1)
                if n == POOL_M0:
                    masked(0)
            for t in range(QT, NT):
                row_scale(1, t, LN_EPS)
            cut_low(2)

            def cut_wo(k):
                c = slice(k * IC // 2, (k + 1) * IC // 2)
                pool.wait_ge(wo_high, 1)
                nc.gpsimd.tensor_tensor(wo_l[:, c, :], wo_s[:, c, :], wo_h[:, c, :].bitcast(fp32),
                                        ALU.subtract).then_inc(wo_low, 1)

            cut_wo(0)
            masked(1)
            cut_low(3)
            cut_wo(1)
            pool.wait_ge(ld_small, 16 * 4)
            pool.wait_ge(misc_fill, MISC_AT[("xT", NT - 1)] + 1)
            addends(0)
            addends(1)
            for c in range(4, IC):
                cut_low(c)
            for t in range(NT):
                row_scale(2, t, FFN_EPS)

        @block.scalar
        def _(act):
            act.wait_ge(consts, 3)
            for s in range(SLOTS):
                act.dma_start(aug[KROWS:KROWS_M, s, 1, :, :], ones_row[:].rearrange("p (o t) -> p o t", o=1
                              ).to_broadcast([2, GH, SQ])).then_inc(ld_ones, 16)

            def take_pre(job):
                kind, k = job
                i = PRE_AT[job]
                act.wait_ge(pre_fill, i + 1)
                bank = ps[:, PRE_RING[i % 4], :]
                if kind == "xT":
                    nc.scalar.copy(xnT[:, :, k * P:(k + 1) * P], bank[:, 0:KC * P].rearrange(
                        "p (c t) -> p c t", c=KC)).then_inc(pre_act, 1)
                elif kind == "v":
                    act.wait_ge(consts, 8)
                    nc.scalar.copy(vaug[:, k, 0:H * VW].rearrange("p (h v) -> p h v", v=VW)[:, :, 0:HD],
                                   bank[:, 0:D].rearrange("p (h d) -> p h d", d=HD)).then_inc(pre_act, 1)
                else:
                    s = CUT_AT[job]
                    if s >= 2:
                        act.wait_ge(scr_done[s % 2], 16 * 3 * (s // 2))
                    nc.scalar.activation(split[:, s % 2, 0, :], bank, ACT.Copy,
                                         scale=SCALE if kind == "q" else 1.0).then_inc(pre_act, 1)

            def middle(job):
                s = CUT_AT[job]
                act.wait_ge(rest_done, s + 1)
                nc.scalar.copy(split[:, s % 2, 1, :], rest[:, s % 2, :]).then_inc(mid_done, 1)

            def maxima(g):
                act.wait_ge(misc_act, act_no(("mT", g)))
                if g >= SLOTS:
                    act.wait_ge(t_fill, 2 * GH * (g - SLOTS + 1))
                for part in range(2):
                    act.dma_start(aug[KROWS + part:KROWS + part + 1, g % SLOTS, 0, :, :],
                                  mrow[part * GH:(part + 1) * GH, g % 2, :]).then_inc(mdma_done[g % 2], 16)

            def take_misc(job):
                kind, k = job
                bank = bank_of(job)
                act.wait_ge(misc_fill, MISC_AT[job] + 1)
                if kind == "mT":
                    if k >= 2:
                        act.wait_ge(mdma_done[k % 2], 32 * (k // 2))
                    nc.scalar.copy(mrow[:, k % 2, :], bank[0:2 * GH, 0:SQ // 2].bitcast(bf16)).then_inc(misc_act, 1)
                    maxima(k)
                elif kind == "xT":
                    nc.scalar.copy(xnT[:, :, k * P:(k + 1) * P], bank[:, 0:KC * P].rearrange(
                        "p (c t) -> p c t", c=KC)).then_inc(misc_act, 1)
                elif kind == "ohT":
                    nc.scalar.copy(ohT[:, k * SQ:(k + 1) * SQ], bank[0:OR, :]).then_inc(misc_act, 1)
                else:
                    if k >= E:
                        act.wait_ge(xm_dve, len(XM_DVE[0]))
                        act.wait_ge(xm_pool, len(XM_POOL[0]))
                    nc.scalar.copy(mk[:, k % E, :], bank).then_inc(misc_act, 1)

            def cut_w1(c):
                act.wait_ge(ld_w1, 16 * E * (c + 1))
                if c >= RW:
                    act.wait_ge(h_fill, UNIT_AT[(c - RW, 1)] + 1)
                nc.scalar.copy(w1h[c % RW][:], w1f[:]).then_inc(w1h_done, 1)

            behind = []
            for job in PRE_A:
                take_pre(job)
                if behind:
                    middle(behind.pop())
                if job[0] in "kq":
                    if job == ("k", 0):
                        behind.append(job)
                    else:
                        middle(job)
            for n in range(LAG):
                for job in OPEN[n]:
                    take_pre(job)
                    if job[0] in "kq":
                        middle(job)
                for job in OPEN_MISC[n]:
                    take_misc(job)

            for n in range(STEPS):
                for job in STEP_MISC[n, 0]:
                    if job[0] in BY_ACT:
                        take_misc(job)
                if n < NH:
                    if n >= PR:
                        act.wait_ge(pv_done, (n - PR) // GH + 1)
                    act.wait_ge(t_fill, 2 * n + 1)
                    nc.scalar.activation(pT[:, n % PR, 0:512], ps[:, T0, :], ACT.Exp).then_inc(t_free, 1)
                    act.wait_ge(t_fill, 2 * n + 2)
                    nc.scalar.activation(pT[:, n % PR, 512:PCOLS], ps[:, T0 + 1:T0 + 3, :].rearrange(
                        "p a b -> p (a b)")[:, 0:PCOLS - 512], ACT.Exp).then_inc(t_free, 1)
                for job in STEP_MISC[n, 1]:
                    if job[0] in BY_ACT:
                        take_misc(job)
                if n == 10:
                    for s in range(2):
                        act.wait_ge(scr_done[s], 16 * 3 * NU)
                    act.wait_ge(picks_done, 1)
                    nc.scalar.copy(sel[:], picks[:]).then_inc(sel_done, 1)
                if n == 18:
                    cut_w1(0)
                if n == 27:
                    cut_w1(1)

            def gelu(i, k=0):
                cols = slice(k * SQ // 2, (k + 1) * SQ // 2) if i == 2 * IC - 1 else slice(0, SQ)
                act.wait_ge(h_fill, i + k + 1)
                if i >= 2:
                    act.wait_ge(gl_done, i - 1)
                nc.scalar.activation(g_ring[:, i % 2, cols], ps[:, h_bank(i, k), cols], ACT.Gelu).then_inc(g_done, 1)

            gelu(0)
            act.wait_ge(pv_done, NG)
            cut_w1(2)
            act.wait_ge(ld_wo, 16)
            nc.scalar.copy(wo_h[:], wo_s[:]).then_inc(wo_high, 1)
            for job in LATE_B[:QT]:
                take_misc(job)
            gelu(1)
            for job in LATE_C + LATE_D:
                take_misc(job)
            for i in range(2, 2 * IC):
                gelu(i)
                c, half = UNITS[i]
                if half == 1 and c + RW < IC:
                    cut_w1(c + RW)
            gelu(2 * IC - 1, 1)

        @block.vector
        def _(dve):
            own = 0

            def stats_of(which, t, src):
                nonlocal own
                nc.vector.bn_stats(stats[:, which, t, :], src[:, t, :]).then_inc(dve_own, 1)
                own += 1
                dve.wait_ge(dve_own, own)
                nc.vector.bn_aggr(mv[:, which, t, :], stats[:, which, t, :]).then_inc(stat_done, 1)

            def normalise(which, src, t, signal):
                dve.wait_ge(rstd_done, which * NT + t + 1)
                nc.vector.tensor_scalar(xn[:, t, :], src[:, t, :], mv[:, which, t, 0:1], rstd[:, which, t:t + 1],
                                        ALU.subtract, ALU.mult).then_inc(signal, 1)

            def remainder(job):
                s = CUT_AT[job]
                dve.wait_ge(pre_act, PRE_AT[job] + 1)
                if s >= 2:
                    dve.wait_ge(low_done, s - 1)
                nc.vector.scalar_tensor_tensor(out=rest[:, s % 2, :], in0=ps[:, PRE_RING[PRE_AT[job] % 4], :],
                                               scalar=SCALE if job[0] == "q" else 1.0, in1=split[:, s % 2, 0, :],
                                               op0=ALU.mult, op1=ALU.subtract).then_inc(rest_done, 1)

            for b in range(B):
                dve.wait_ge(ld_x[b], 16)
                for t in range(b * QT, (b + 1) * QT):
                    stats_of(0, t, xs)
                if b == 0:
                    remainder(("k", 0))
                for t in range(b * QT, (b + 1) * QT):
                    normalise(0, xs, t, xn_done)
                if b == 0:
                    for job in (("q", 0), ("k", 1), ("q", 1)):
                        remainder(job)

            DEFER = 1
            dve.wait_ge(consts, 5)

            def head_max(n):
                g, j = n // GH, n % GH
                for k, tiles in enumerate(((3,), (2, 0), (1,))):
                    dve.wait_ge(s_fill, 3 * n + k + 1)
                    for qt in tiles:
                        c = S_COL[qt]
                        scores = ps[:, S0 + c // 512, c % 512:c % 512 + S_LEN[qt]]
                        last = nc.vector.tensor_tensor_reduce(
                            out=scores, in0=scores, in1=mask[:, SQ - S_LEN[qt]:SQ], scale=1.0, scalar=NEG,
                            op0=ALU.add, op1=ALU.max, accum_out=mmax[:, g % 2, qt, j:j + 1])
                    last.then_inc(s_free, 1)
                if j == GH - 1:
                    if g >= 2:
                        dve.wait_ge(misc_fill, MISC_AT[("mT", g - 2)] + 1)
                    dve.wait_ge(s_free, 3 * n + 3)
                    nc.vector.tensor_scalar(mparts[:, g % 2, :, 0, :], mmax[:, g % 2, :, :], -1.0, None,
                                            ALU.mult).then_inc(m_high, 1)
                    dve.wait_ge(m_high, g + 1)
                    nc.vector.scalar_tensor_tensor(out=mparts[:, g % 2, :, 1, :], in0=mmax[:, g % 2, :, :],
                                                   scalar=-1.0, in1=mparts[:, g % 2, :, 0, :],
                                                   op0=ALU.mult, op1=ALU.subtract).then_inc(m_done, 1)

            def norm_group(g):
                nonlocal own
                dve.wait_ge(pv_done, g + 1)
                dve.wait_ge(dve_own, own)
                if g >= 2:
                    dve.wait_ge(on_done, g // 2)
                nc.vector.transpose(oq[:, 0, :, :].rearrange("p a b -> p (a b)"), ps[:, PO, :]).then_inc(o_taken, 1)
                dve.wait_ge(o_taken, g + 1)
                nc.vector.reciprocal(rsum[:], oq[:, 0, :, HD]).then_inc(dve_own, 1)
                own += 1
                dve.wait_ge(dve_own, own)
                side = slice(g % 2 * HD, (g % 2 + 1) * HD)
                nc.vector.tensor_tensor(oq[:, 1, :, side], oq[:, 0, :, 0:HD], rsum[:].rearrange(
                    "p (a o) -> p a o", o=1).to_broadcast([P, SQ // BK, HD]), ALU.mult).then_inc(dve_own, 1)
                own += 1
                if g % 2:
                    if g >= GB:
                        dve.wait_ge(misc_fill, MISC_AT[("x1", QT - 1)] + 1)
                    dve.wait_ge(dve_own, own)
                    nc.vector.transpose(onT[:, g % GB // 2, :], oq[:, 1, :, :].rearrange("p a b -> p (a b)")
                                        ).then_inc(on_done, 1)

            def one_hot(b, bank):
                ts = slice(b * QT, (b + 1) * QT)
                nc.vector.tensor_copy(lg[:, ts, :], bank[:, 0:QT * E].rearrange("p (t e) -> p t e", e=E)
                                      ).then_inc(misc_dve, 1)
                dve.wait_ge(misc_dve, dve_no(("logits", b)))

                def step(k):
                    dve.wait_ge(oh_step, 5 * b + k)

                def spread(m):
                    return m[:, ts].rearrange("p (t o) -> p t o", o=1).to_broadcast([P, QT, E])

                nc.vector.tensor_reduce(lmax[:, ts], lg[:, ts, :], mybir.AxisListType.X, ALU.max).then_inc(oh_step, 1)
                step(1)
                nc.vector.tensor_tensor(lg[:, ts, :], lg[:, ts, :], spread(lmax), ALU.is_equal).then_inc(oh_step, 1)
                step(2)
                nc.vector.tensor_tensor(lg[:, ts, :], lg[:, ts, :], pri[:].rearrange(
                    "p (o e) -> p o e", o=1).to_broadcast([P, QT, E]), ALU.mult).then_inc(oh_step, 1)
                step(3)
                nc.vector.tensor_reduce(lmax[:, ts], lg[:, ts, :], mybir.AxisListType.X, ALU.max).then_inc(oh_step, 1)
                step(4)
                nc.vector.tensor_tensor(oh[:, :, BK:BK + E], lg[:, ts, :], spread(lmax), ALU.is_equal)
                nc.vector.tensor_tensor(oh[:, :, 0:E], lg[:, ts, :], spread(lmax), ALU.is_equal).then_inc(oh_step, 1)

            def take_misc(job):
                kind, k = job
                bank = bank_of(job)
                dve.wait_ge(misc_fill, MISC_AT[job] + 1)
                if kind == "x1":
                    nc.vector.tensor_tensor(xs[:, k, :], xs[:, k, :], bank[:, 0:D], ALU.add).then_inc(misc_dve, 1)
                    dve.wait_ge(misc_dve, dve_no(job))
                    stats_of(1, k, xs)
                    if k % QT:
                        normalise(1, xs, k - 1, xn_done)
                    if k % QT == QT - 1:
                        normalise(1, xs, k, xn_done)
                elif kind == "logits":
                    one_hot(k, bank)

            def cut_x(b):
                if b:
                    dve.wait_ge(xm_dve, len(XM_DVE[0]))
                    dve.wait_ge(xm_pool, len(XM_POOL[0]))
                else:
                    dve.wait_ge(sel_done, 1)
                    dve.wait_ge(ld_ones, 16 * SLOTS)
                dve.wait_ge(misc_act, act_no(("xT", b * QT + QT - 1)))
                nc.vector.tensor_copy(xh[:], xnT[:, :, b * SQ:(b + 1) * SQ]).then_inc(x_parts, 1)
                dve.wait_ge(x_parts, 2 * b + 1)
                nc.vector.tensor_tensor(xl[:], xnT[:, :, b * SQ:(b + 1) * SQ], xh[:].bitcast(fp32),
                                        ALU.subtract).then_inc(x_parts, 1)

            def masked(b):
                dve.wait_ge(x_parts, 2 * (b + 1))
                for e, part in XM_DVE[b]:
                    dve.wait_ge(misc_act, act_no(("mk", E * b + e)))
                    nc.vector.tensor_tensor(xmT[b][part][:, e, :, :], (xh, xl)[part][:].bitcast(fp32), spread_mask(e),
                                            ALU.mult).then_inc(xm_dve, 1)

            for n in range(LAG):
                head_max(n)
                for job in OPEN.get(n - DEFER, ()):
                    if job[0] in "kq":
                        remainder(job)
            for n in range(STEPS):
                if n + LAG < NH:
                    head_max(n + LAG)
                for job in STEP_MISC[n, 0] + STEP_MISC[n, 1]:
                    if job[0] in BY_DVE:
                        take_misc(job)
                if n >= GH + 2 and n % GH == 2:
                    norm_group((n - GH - 2) // GH)
                if n == DVE_M0:
                    cut_x(0)
                    masked(0)
                if n == 24:
                    dve.wait_ge(ld_b1, 32)
                    nc.vector.tensor_copy(b1s[:], b1f[:]).then_inc(dve_own, 1)
                    own += 1
                    dve.wait_ge(dve_own, own)
                    nc.vector.tensor_tensor(b1s[BK:2 * BK, :], b1f[BK:2 * BK, :], b1s[BK:2 * BK, :].bitcast(fp32),
                                            ALU.subtract
                                            ).then_inc(b1_done, 1)
            def cut_g(i, k=0):
                cols = slice(k * SQ // 2, (k + 1) * SQ // 2) if i == 2 * IC - 1 else slice(0, SQ)
                dve.wait_ge(g_done, i + k + 1)
                if i >= 2:
                    dve.wait_ge(y_done, QT * (i - 1))
                nc.vector.tensor_copy(g_h[:, i % 2, cols], g_ring[:, i % 2, cols]).then_inc(gh_done, 1)
                dve.wait_ge(gh_done, i + k + 1)
                nc.vector.tensor_tensor(g_l[:, i % 2, cols], g_ring[:, i % 2, cols],
                                        g_h[:, i % 2, cols].bitcast(fp32), ALU.subtract).then_inc(gl_done, 1)

            norm_group(NG - 1)
            cut_g(0)
            for job in LATE_A:
                take_misc(job)
            cut_x(1)
            take_misc(("logits", 1))
            cut_g(1)
            masked(1)
            for i in range(2, END0 + 2):
                cut_g(i)

            dve.wait_ge(ld_small, 16 * 4)
            dve.wait_ge(xb_done, 2 * B)

            def sum_up(t):
                nonlocal own
                dve.wait_ge(y_done, QT * UNIT_AT[(IC - 1, t // QT)] + t % QT // 2 * 2 + 2)
                nc.vector.tensor_tensor(xn[:, t, :], ybank(t), xn[:, t, :], ALU.add).then_inc(dve_own, 1)
                own += 1
                dve.wait_ge(dve_own, own)
                stats_of(2, t, xn)

            def finish(t):
                nonlocal own
                dve.wait_ge(stat_done, 2 * NT + t + 1)
                nc.vector.scalar_tensor_tensor(out=xn[:, t, :], in0=xn[:, t, :], scalar=mv[:, 2, t, 0:1], in1=gam[:],
                                               op0=ALU.subtract, op1=ALU.mult).then_inc(dve_own, 1)
                own += 1
                dve.wait_ge(dve_own, own)
                dve.wait_ge(rstd_done, 2 * NT + t + 1)
                nc.vector.scalar_tensor_tensor(out=xn[:, t, :], in0=xn[:, t, :], scalar=rstd[:, 2, t:t + 1],
                                               in1=xs[:, t, :], op0=ALU.mult, op1=ALU.add).then_inc(z_done, 1)

            def last_tiles(first, end):
                for t in range(first, end + 1):
                    if t < end:
                        sum_up(t)
                    if t > first:
                        finish(t - 1)

            last_tiles(0, QT // 2)
            cut_g(END0 + 2)
            last_tiles(QT // 2, QT)
            for i in range(END0 + 3, 2 * IC - 1):
                cut_g(i)
            for k in range(2):
                cut_g(2 * IC - 1, k)
            last_tiles(QT, NT)

        @block.tensor
        def _(pe):
            def pre(job):
                kind, k = job
                i = PRE_AT[job]
                if i >= 4:
                    if PRE[i - 4][0] in "kq":
                        pe.wait_ge(rest_done, CUT_AT[PRE[i - 4]] + 1)
                    else:
                        pe.wait_ge(pre_act, i - 3)
                bank = ps[:, PRE_RING[i % 4], :]
                if kind == "xT":
                    pe.wait_ge(consts, 4)
                    pe.wait_ge(xn_done, k + 1)
                    for c in range(KC):
                        last = nc.tensor.transpose(bank[:, c * P:(c + 1) * P], xn[:, k, c * P:(c + 1) * P], ident[:])
                elif kind == "v":
                    pe.wait_ge(ld_wv, 16)
                    for c in range(KC):
                        last = nc.tensor.matmul(bank[:, 0:D], ctxT_s[:, c, k // QT, k % QT * P:(k % QT + 1) * P],
                                                wqkv[:, 2, c, :], start=(c == 0), stop=(c == KC - 1))
                else:
                    b, j = k // KC, "qk".index(kind)
                    if kind == "q":
                        pe.wait_ge(ld_wq, 16)
                        pe.wait_ge(pre_act, PRE_AT[("xT", b * QT + QT - 1)] + 1)
                    else:
                        pe.wait_ge(ld_wk, 16)
                        pe.wait_ge(ld_ctx[b], 16)
                    for c in range(KC):
                        src = ctxT_s[:, c, b, :] if kind == "k" else xnT[:, c, b * SQ:(b + 1) * SQ]
                        last = nc.tensor.matmul(bank, wqkv[:, j, c, k % KC * P:(k % KC + 1) * P], src,
                                                start=(c == 0), stop=(c == KC - 1))
                last.then_inc(pre_fill, 1)

            def scores(n):
                g, h = n // GH, n % GH
                if h == 0:
                    pe.wait_ge(aug_done[g % SLOTS], 16 * (len(RUNS_Q) + len(RUNS_K)) * (g // SLOTS + 1))
                for k, tiles in enumerate(((3,), (2, 0), (1,))):
                    if n >= 1:
                        pe.wait_ge(s_free, 3 * (n - 1) + k + 1)
                    for qt in tiles:
                        c = S_COL[qt]
                        last = nc.tensor.matmul(ps[:, S0 + c // 512, c % 512:c % 512 + S_LEN[qt]],
                                                aug[0:KROWS, g % SLOTS, 0, h, qt * P:(qt + 1) * P],
                                                aug[0:KROWS, g % SLOTS, 1, h, 0:S_LEN[qt]], start=True, stop=True)
                    last.then_inc(s_fill, 1)

            def scores_T(n):
                g, h = n // GH, n % GH
                if h == 0:
                    pe.wait_ge(mdma_done[g % 2], 32 * (g // 2 + 1))
                for k, tiles in enumerate(((0,), (1, 3), (2,))):
                    if n >= 1 and k < 2:
                        pe.wait_ge(t_free, 2 * (n - 1) + k + 1)
                    for kt in tiles:
                        c = T_COL[kt]
                        last = nc.tensor.matmul(ps[:, T0 + c // 512, c % 512:c % 512 + T_LEN[kt]],
                                                aug[0:KROWS_M, g % SLOTS, 1, h, kt * P:(kt + 1) * P],
                                                aug[0:KROWS_M, g % SLOTS, 0, h, kt * P:SQ], start=True, stop=True)
                    if k != 1:
                        last.then_inc(t_fill, 1)

            def weigh(g, tiles):
                if tiles[0] == 0:
                    pe.wait_ge(p_masked, GH * (g + 1))
                    if g >= 1:
                        pe.wait_ge(o_taken, g)
                b = g // GB
                for kt in tiles:
                    for j in range(GH):
                        n = g * GH + j
                        v0 = n % H * VW
                        last = nc.tensor.matmul(ps[BK * j:BK * j + BK, PO, kt * P:SQ],
                                                vaug[:, b * QT + kt, v0:v0 + BK],
                                                pT[:, n % PR, T_COL[kt]:T_COL[kt] + T_LEN[kt]],
                                                start=(kt == 0), stop=(kt == QT - 1), skip_group_check=True)
                if tiles[-1] == QT - 1:
                    last.then_inc(pv_done, 1)

            def misc(job):
                kind, k = job
                i = MISC_AT[job]
                bank = bank_of(job)
                if MISC_BANK[i] < T0:
                    pe.wait_ge(s_free, 3 * NH)
                before = [m for m in MISC[:i] if MISC_BANK[MISC_AT[m]] == MISC_BANK[i]]
                if before:
                    if before[-1][0] in BY_DVE:
                        pe.wait_ge(misc_dve, dve_no(before[-1]))
                    else:
                        pe.wait_ge(misc_act, act_no(before[-1]))
                if kind == "mT":
                    pe.wait_ge(m_done, k + 1)
                    for qt in range(QT):
                        last = nc.tensor.transpose(bank[0:2 * GH, qt * P // 2:(qt + 1) * P // 2].bitcast(bf16),
                                                   mparts[:, k % 2, qt, :, :].rearrange("p a b -> p (a b)"),
                                                   identb[:])
                elif kind == "x1":
                    pe.wait_ge(on_done, GB // 2 * (k // QT + 1))
                    pe.wait_ge(ld_woT, 16 * 2 * GH)
                    for g in range(GB // 2):
                        last = nc.tensor.matmul(bank[:, 0:D], onT[:, g, k % QT * P:(k % QT + 1) * P],
                                                wo_att[:, g, :], start=(g == 0), stop=(g == GB // 2 - 1))
                elif kind == "xT":
                    pe.wait_ge(xn_done, NT + k + 1)
                    for c in range(KC):
                        last = nc.tensor.transpose(bank[:, c * P:(c + 1) * P], xn[:, k, c * P:(c + 1) * P], ident[:])
                elif kind == "logits":
                    pe.wait_ge(ld_small, 16 * 4)
                    pe.wait_ge(misc_act, act_no(("xT", k * QT + QT - 1)))
                    for t in range(k * QT, (k + 1) * QT):
                        for c in range(KC):
                            last = nc.tensor.matmul(bank[:, t % QT * E:(t % QT + 1) * E],
                                                    xnT[:, c, t * P:(t + 1) * P], wr_s[:, c, :],
                                                    start=(c == 0), stop=(c == KC - 1))
                elif kind == "ohT":
                    pe.wait_ge(oh_step, 5 * (k + 1))
                    for j in range(QT):
                        last = nc.tensor.transpose(bank[0:OR, j * P:(j + 1) * P], oh[:, j, :], ident[:])
                else:
                    b, e = k // E, k % E
                    pe.wait_ge(sel_done, 1)
                    pe.wait_ge(misc_act, act_no(("ohT", b)))
                    last = nc.tensor.matmul(bank, sel[:, e, :], ohT[:, b * SQ:(b + 1) * SQ], start=True, stop=True)
                last.then_inc(misc_fill, 1)

            for job in PRE_A:
                pre(job)
            pe.wait_ge(consts, 6)
            for n in range(LAG):
                if n > 0:
                    scores(n)
                for job in OPEN[n]:
                    pre(job)
                if n == 0:
                    scores(n)
                for job in OPEN_MISC[n]:
                    misc(job)
            pe.wait_ge(pre_act, len(PRE))
            pe.wait_ge(rest_done, 2 * NU)
            pe.wait_ge(ld_ones, 16 * SLOTS)
            def hidden(i, experts=range(E), k2=None):
                c, half = UNITS[i]
                cols = slice(0, SQ) if k2 is None else slice(k2 * SQ // 2, (k2 + 1) * SQ // 2)
                bank = ps[:, h_bank(i, k2 or 0), cols]
                if experts[0] == 0:
                    pe.wait_ge(w1l_done, c + 1)
                    if i >= 3:
                        pe.wait_ge(g_done, i - 2 + (k2 or 0))
                    nc.tensor.matmul(bank, b1s[:, c * P:(c + 1) * P], ohT[:, half * SQ + cols.start:half * SQ + cols.stop],
                                     start=True, stop=False)
                high, low = w1h[c % RW], w1l[c % RW]
                for e in experts:
                    if c == 0:
                        for made, mine in ((xm_dve, XM_DVE), (xm_pool, XM_POOL)):
                            upto = [j for j, (ex, _) in enumerate(mine[half]) if ex == e]
                            if upto:
                                pe.wait_ge(made, half * len(mine[0]) + upto[-1] + 1)
                    for k in range(KC):
                        for w, part in ((high, 0), (low, 0), (high, 1)):
                            end = e == E - 1 and k == KC - 1 and part == 1
                            last = nc.tensor.matmul(bank, w[:, e, k, :], xmT[half][part][:, e, k, cols],
                                                    start=False, stop=end)
                if end:
                    last.then_inc(h_fill, 1)

            for n in range(STEPS):
                if n + LAG < NH:
                    scores(n + LAG)
                for job in STEP_MISC[n, 0]:
                    misc(job)
                if n < NH:
                    scores_T(n)
                for job in STEP_MISC[n, 1]:
                    misc(job)
                if n >= GH and n % GH == 0:
                    weigh(n // GH - 1, (0, 1))
                if n >= GH and n % GH == 1:
                    weigh(n // GH - 1, (2, 3))
                if n in HID_AT:
                    if n == HID_AT[0]:
                        pe.wait_ge(b1_done, 1)
                        pe.wait_ge(misc_act, act_no(("mk", E - 1)))
                    hidden(0, [HID_AT.index(n)])

            def share(i):
                c, half = UNITS[i]
                pe.wait_ge(gl_done, i + 1)
                pe.wait_ge(wo_low, 1 if c < IC // 2 else 2)
                for j in range(QT):
                    if i == 2 * IC - 1 and j == QT // 2:
                        pe.wait_ge(gl_done, i + 2)
                    for g, w in ((g_h, wo_h), (g_l, wo_h), (g_h, wo_l)):
                        last = nc.tensor.matmul(ybank(half * QT + j), g[:, i % 2, j * P:(j + 1) * P], w[:, c, :],
                                                start=(c == 0 and j % 2 == 0 and w is wo_h and g is g_h),
                                                stop=(c == IC - 1 and w is wo_l), skip_group_check=True)
                    last.then_inc(y_done, 1)

            hidden(1, range(0, 2))
            pe.wait_ge(t_free, 2 * NH)
            pe.wait_ge(o_taken, NG)
            for job in LATE_A:
                misc(job)
            hidden(1, range(2, E))
            share(0)
            for job in LATE_B:
                misc(job)
            hidden(2)
            for job in LATE_C:
                misc(job)
            share(1)
            for job in LATE_D:
                misc(job)
            for i in range(3, 2 * IC - 1):
                hidden(i)
                share(i - 1)
            hidden(2 * IC - 1, k2=0)
            share(2 * IC - 2)
            hidden(2 * IC - 1, k2=1)
            share(2 * IC - 1)


def kernel(x, ctx_1024, L0_xattn_Wq, L0_xattn_Wk, L0_xattn_Wv, L0_xattn_Wo, L0_ffn_W_router, L0_ffn_W1, L0_ffn_b1,
           L0_ffn_Wo, L0_ffn_bo, L0_ffn_ln_gamma, L0_ffn_ln_beta):
    import numpy as np
    import concourse.bacc as bacc
    from concourse import mybir
    from concourse.bass_utils import run_bass_kernel_spmd

    laid = {
        "x": x, "ctxT": np.transpose(ctx_1024, (0, 2, 1)),
        "wqT": np.transpose(L0_xattn_Wq), "wkT": np.transpose(L0_xattn_Wk), "wvT": np.transpose(L0_xattn_Wv),
        "woT": np.transpose(L0_xattn_Wo), "w_router": L0_ffn_W_router, "w1": L0_ffn_W1, "b1": L0_ffn_b1,
        "wo": L0_ffn_Wo, "bo": L0_ffn_bo, "gamma": L0_ffn_ln_gamma, "beta": L0_ffn_ln_beta,
    }
    nc = bacc.Bacc("TRN2", target_bir_lowering=False, num_devices=1)
    arrays, aps = {}, []
    for name, a in laid.items():
        a = np.ascontiguousarray(a)
        arrays[f"in_{name}"] = a
        aps.append(nc.dram_tensor(f"in_{name}", a.shape, mybir.dt.from_np(a.dtype), kind="ExternalInput").ap())
    out = nc.dram_tensor("out_x", arrays["in_x"].shape, mybir.dt.float32, kind="ExternalOutput").ap()
    cross_attention_moe_ffn(nc, *aps, out)
    r = run_bass_kernel_spmd(nc, [arrays], core_ids=[0])
    return r.results[0]["out_x"]
```

```python
import concourse.bass as bass
from concourse import mybir
from contextlib import ExitStack


def cross_attention_moe_ffn(nc: bass.Bass, x, ctxT, wqT, wkT, wvT, woT, w_router, w1, b1, wo, bo, gamma, beta, out):
    fp32, bf16, f32r = mybir.dt.float32, mybir.dt.bfloat16, mybir.dt.float32r
    ALU, ACT = mybir.AluOpType, mybir.ActivationFunctionType

    P = 128
    B, SQ, D = x.shape
    HD = 16
    H = D // HD
    SCALE = HD ** -0.5
    KC = D // P
    QT = SQ // P
    NT = B * QT
    HU = P // HD
    NU = B * KC
    GH = 4
    NG = B * H // GH
    GB = NG // B
    NH = B * H
    BK = 32
    E, _, I = w1.shape
    IC = I // P
    LN_EPS, FFN_EPS = 1e-5, 1e-12
    RUNS_Q = ((0, 1), (0, 1, 2), (0,))
    RUNS_K = ((0, 1, 2), (0,), (0, 1))
    KROWS = HD * sum(len(r) for r in RUNS_Q)
    KROWS_M = KROWS + 2
    PCOLS = P * QT * (QT + 1) // 2
    VW = HD + 1
    OR = 3 * BK
    NEG = -1.0e30
    SLOTS = 4
    RS = 4
    PR = 8
    RW = 3

    LAG = 7
    WEIGH = ((0,), (1,), (2, 3), ())
    NORM_AT = 3
    BACK = 1
    ATTN_TAIL = 3
    MT_PLACE = 1
    X1_AT = 2
    HALF0_REST = [[], [("logits", 0)], [], [("ohT", 0)], [], [("mk", e) for e in range(E)]]
    CUT_X_AT = (25, 26)
    DVE_M0, POOL_M0 = 27, 27
    ACT_W1, POOL_W1 = (14, 22), (16, 24)
    SEL_AT, B1_AT, B1_LOW_AT = 10, 8, 25
    HID_AT = (30, 30, 31, 31)
    HID1_A = 2
    AHEAD = 3

    ctx = ExitStack()
    with ctx:
        SBUF_BASE = 16512
        place = {"next": SBUF_BASE}

        def width(shape, dt):
            n = mybir.dt.size(dt)
            for d in shape[1:]:
                n *= d
            return -(-n // 32) * 32

        def sb(name, shape, dt=fp32):
            at = place["next"]
            place["next"] = at + width(shape, dt)
            place[name] = at
            return nc.alloc_sbuf_tensor_at(name, shape, dt, offset=at)

        def over(name, shape, dt, first, skip=0):
            return nc.alloc_sbuf_tensor_at(name, shape, dt, offset=place[first] + skip)

        def sem(name):
            return ctx.enter_context(nc.semaphore(name))

        xs = sb("xs", [P, NT, D])
        xn = sb("xn", [P, NT, D])
        xnT = sb("xnT", [P, B, KC, SQ])
        XT = 4 * KC * SQ
        xhl = [[over(f"xh{b}", [P, KC, SQ], f32r, "xnT", (1 - b) * XT),
                over(f"xl{b}", [P, KC, SQ], f32r, "xnT", b * XT)] for b in range(B)]
        ctxT_s = sb("ctxT_s", [P, KC, B, SQ])
        w1f = over("w1f", [P, E, KC, P], fp32, "ctxT_s")
        b1f = over("b1f", [OR, I], fp32, "ctxT_s", 4 * E * KC * P)
        wqkv = sb("wqkv", [P, 3, KC, D])
        mk = over("mk", [P, E, SQ], bf16, "wqkv")
        wo_att = sb("wo_att", [P, GB // 2, D])
        vaug = sb("vaug", [P, NT, H * VW + BK - VW])
        aug = sb("aug", [P, SLOTS, 2, GH, SQ], bf16)
        pT = sb("pT", [P, PR, PCOLS])
        XB = E * KC * SQ * 4
        xmT0h, xmT0l = sb("xmT0h", [P, E, KC, SQ], f32r), sb("xmT0l", [P, E, KC, SQ], f32r)
        xmT1h, xmT1l = over("xmT1h", [P, E, KC, SQ], f32r, "aug"), over("xmT1l", [P, E, KC, SQ], f32r, "aug", XB)
        xmT = ((xmT0h, xmT0l), (xmT1h, xmT1l))
        split = over("split", [P, 2 * NU, 3, SQ], bf16, "xmT0h")
        rest = over("rest", [P, RS, SQ], fp32, "xmT0h", 2 * NU * 3 * SQ * 2)
        ohT = sb("ohT", [OR, B * SQ], f32r)
        sel = over("sel", [OR, E, P], f32r, "wqkv", 2 * E * SQ)
        b1s = sb("b1s", [OR, I], f32r)
        oq = sb("oq", [P, 2, SQ // BK, BK])
        onT = sb("onT", [P, GB // 2, SQ])
        WB = E * KC * P * 4
        w1h = [sb("w1h0", [P, E, KC, P], f32r), sb("w1h1", [P, E, KC, P], f32r),
               over("w1h2", [P, E, KC, P], f32r, "pT")]
        w1l = [sb("w1l0", [P, E, KC, P], f32r), sb("w1l1", [P, E, KC, P], f32r),
               over("w1l2", [P, E, KC, P], f32r, "pT", WB)]
        GW = 4 * 2 * SQ
        g_ring = sb("g_ring", [P, 2, SQ])
        g_h = over("g_h", [P, 2, SQ], f32r, "pT", 2 * WB)
        g_l = over("g_l", [P, 2, SQ], f32r, "pT", 2 * WB + GW)
        wo_h = over("wo_h", [P, IC, D], f32r, "pT", 2 * WB + 2 * GW)
        wo_l = over("wo_l", [P, IC, D], f32r, "vaug")
        wo_s = sb("wo_s", [P, IC, D])
        wr_s = sb("wr_s", [P, KC, E])
        gam = sb("gam", [P, D])
        bet = sb("bet", [P, D])
        bo_s = sb("bo_s", [P, D])
        mask = sb("mask", [P, SQ], bf16)
        ones_sq = over("ones_sq", [P, P], fp32, "g_ring")
        ident = sb("ident", [P, P])
        identb = sb("identb", [P, P], bf16)
        ones_row = over("ones_row", [2, SQ], bf16, "g_ring", 4 * P)
        picks = over("picks", [OR, E, P], fp32, "g_ring", 4 * P + 2 * SQ)
        mhalf = sb("mhalf", [P, 1])
        mmax = sb("mmax", [P, 2, QT, GH])
        mparts = sb("mparts", [P, 2, QT, 2, GH], bf16)
        mrow = sb("mrow", [2 * GH, 2, SQ], bf16)
        rsum = sb("rsum", [P, SQ // BK])
        stats = sb("stats", [P, 3, NT, 6])
        mv = sb("mv", [P, 3, NT, 2])
        veps = sb("veps", [P, 3, NT])
        rstd = sb("rstd", [P, 3, NT])
        lg = sb("lg", [P, NT, E])
        lmax = sb("lmax", [P, NT])
        pri = sb("pri", [P, E])
        oh = sb("oh", [P, QT, OR])

        ps = ctx.enter_context(nc.psum_tensor("ps", [P, 8, 512], fp32))
        S0, T0, PO, PM = 0, 3, 6, 7
        H_RING = (0, 1, 2)

        def h_bank(i, k=0):
            return H_RING[(i + k) % 3]

        def ybank(t):
            return ps[:, 3 + t // 2, t % 2 * D:(t % 2 + 1) * D]

        ld_x = [sem(f"ld_x{b}") for b in range(B)]
        ld_ctx = [sem(f"ld_ctx{b}") for b in range(B)]
        ld_wq, ld_wk, ld_wv = sem("ld_wq"), sem("ld_wk"), sem("ld_wv")
        ld_small, ld_woT, ld_b1, ld_wo, ld_w1 = (sem(n) for n in ("ld_small", "ld_woT", "ld_b1", "ld_wo", "ld_w1"))
        ld_ones = sem("ld_ones")
        consts = sem("consts")
        pool_own = sem("pool_own")
        dve_own = sem("dve_own")
        stat_done = sem("stat_done")
        rstd_done = sem("rstd_done")
        xn_done = sem("xn_done")
        xn_pool = sem("xn_pool")
        pre_fill = sem("pre_fill")
        pre_act = sem("pre_act")
        rest_done = sem("rest_done")
        mid_done = sem("mid_done")
        low_done = sem("low_done")
        scr_done = [sem(f"scr_done{s}") for s in range(2 * NU)]
        aug_done = [sem(f"aug_done{s}") for s in range(SLOTS)]
        s_fill = sem("s_fill")
        s_free = sem("s_free")
        m_high = sem("m_high")
        m_done = sem("m_done")
        mdma_done = [sem("mdma_done0"), sem("mdma_done1")]
        t_fill = sem("t_fill")
        t_free = sem("t_free")
        p_masked = sem("p_masked")
        pv_done = sem("pv_done")
        o_taken = sem("o_taken")
        rsum_done = sem("rsum_done")
        scaled = sem("scaled")
        on_done = sem("on_done")
        misc_fill = sem("misc_fill")
        misc_act = sem("misc_act")
        misc_dve = sem("misc_dve")
        oh_step = sem("oh_step")
        picks_done = sem("picks_done")
        sel_done = sem("sel_done")
        x_parts = sem("x_parts")
        xm_dve = sem("xm_dve")
        xm_pool = sem("xm_pool")
        wo_high = sem("wo_high")
        wo_low = sem("wo_low")
        gh_done = sem("gh_done")
        gl_done = sem("gl_done")
        b1_zero = sem("b1_zero")
        b1_done = sem("b1_done")
        w1h_done = sem("w1h_done")
        w1l_done = sem("w1l_done")
        h_fill = sem("h_fill")
        g_done = sem("g_done")
        y_done = sem("y_done")
        xb_done = sem("xb_done")
        z_done = sem("z_done")
        out_done = sem("out_done")

        scr = nc.dram_tensor("parts_scratch", (2 * NU, HU, 3, HD, SQ), bf16, kind="Internal").ap()

        PRE_A = [("xT", t) for t in range(QT)] + [("k", 0), ("q", 0), ("k", 1)] + [("xT", t) for t in range(QT, NT)] + [
            ("q", 1), ("k", 2), ("k", 3)]
        OPEN = {0: [("q", 2)], 1: [("q", 3)], 2: [("v", 0), ("v", 1)], 3: [("v", 2), ("v", 3)],
                4: [("v", 4), ("v", 5)], 5: [("v", 6), ("v", 7)], 6: []}
        PRE = PRE_A + [j for n in range(LAG) for j in OPEN[n]]
        PRE_AT = {j: i for i, j in enumerate(PRE)}
        PRE_BANK = [3 + i % 5 for i in range(len(PRE_A))] + [3 + i % 4 for i in range(len(PRE) - len(PRE_A))]
        CUTS = [j for j in PRE if j[0] in "kq"]
        CUT_AT = {j: i for i, j in enumerate(CUTS)}

        SP_OPEN = [("k", 0, 0), ("q", 0, 0), ("k", 0, 1), ("k", 0, 2), ("q", 0, 1), ("k", 1, 0), ("q", 0, 2),
                   ("stack", "k", 0), ("stack", "q", 0), ("k", 1, 1), ("q", 1, 0), ("k", 1, 2), ("q", 1, 1),
                   ("q", 1, 2), ("k", 2, 0), ("stack", "k", 1), ("k", 2, 1), ("stack", "q", 1),
                   ("k", 2, 2), ("k", 3, 0), ("k", 3, 1), ("k", 3, 2), ("stack", "k", 2), ("stack", "q", 2),
                   ("q", 2, 0), ("q", 2, 1), ("q", 2, 2), ("maxima", 0), ("stack", "k", 3), ("stack", "q", 3),
                   ("q", 3, 0), ("q", 3, 1), ("q", 3, 2), ("maxima", 1)]

        STEPS = NH + ATTN_TAIL
        assert max(HID_AT) < STEPS
        OPEN_MISC = {n: [] for n in range(LAG)}
        STEP_MISC = {(n, w): [] for n in range(STEPS) for w in range(2)}
        for g in range(NG):
            n = GH * g + GH - LAG
            if n >= 0:
                STEP_MISC[n, MT_PLACE].append(("mT", g))
            else:
                OPEN_MISC[n + LAG].append(("mT", g))
        at = 2 * (GB * GH + NORM_AT + BACK) + X1_AT
        for i, jobs in enumerate([[("x1", t)] for t in range(QT)] + [[("xT", t)] for t in range(QT)] + HALF0_REST):
            STEP_MISC[(at + i) // 2, (at + i) % 2] += jobs
        LATE_A = [("x1", t) for t in range(QT, NT)]
        LATE_B = [("xT", t) for t in range(QT, NT)] + [("logits", 1)]
        LATE_C = [("ohT", 1)]
        LATE_D = [("mk", i) for i in range(E, 2 * E)]
        MISC = [j for n in range(LAG) for j in OPEN_MISC[n]] + [
            j for n in range(STEPS) for w in range(2) for j in STEP_MISC[n, w]]
        free = [j for n in range(NH - LAG, STEPS) for w in range(2) for j in STEP_MISC[n, w]]
        MISC_BANK = [PM] * (len(MISC) - len(free)) + [(0, 1, 2, PM)[i % 4] for i in range(len(free))]
        LATE = LATE_A + LATE_B + LATE_C + LATE_D
        MISC_BANK += [(PM, 5, PO)[i % 3] for i in range(len(LATE))]
        MISC += LATE
        MISC_AT = {j: i for i, j in enumerate(MISC)}
        BY_ACT, BY_DVE = ("mT", "xT", "ohT", "mk"), ("x1", "logits")

        def act_no(job):
            return sum(k in BY_ACT for k, _ in MISC[:MISC_AT[job] + 1])

        def dve_no(job):
            return sum(k in BY_DVE for k, _ in MISC[:MISC_AT[job] + 1])

        XM_DVE = {0: [(0, 0), (0, 1), (1, 0), (1, 1), (2, 0), (2, 1)], 1: [(0, 0), (0, 1), (1, 0), (2, 0), (2, 1)]}
        XM_POOL = {0: [(3, 0), (3, 1)], 1: [(1, 1), (3, 0), (3, 1)]}

        def scale_operands(g):
            side = slice(g % 2 * HD, (g % 2 + 1) * HD)
            return oq[:, 1, :, side], oq[:, 0, :, 0:HD], rsum[:].rearrange(
                "p (a o) -> p a o", o=1).to_broadcast([P, SQ // BK, HD])

        def spread_mask(e):
            return mk[:, e, :].rearrange("p (o t) -> p o t", o=1).to_broadcast([P, KC, SQ])

        def bank_of(job):
            return ps[:, MISC_BANK[MISC_AT[job]], :]

        MIDDLE = [(c, h) for c in range(RW, IC - AHEAD) for h in range(2)]
        UNITS = [(c, h) for h in range(2) for c in range(RW)] + MIDDLE + [
            (c, h) for h in range(2) for c in range(IC - AHEAD, IC)]
        UNIT_AT = {u: i for i, u in enumerate(UNITS)}
        END0 = UNIT_AT[(IC - 1, 0)]

        T_COL = {0: 0, 1: 512, 3: 896, 2: 1024}
        T_LEN = {kt: (QT - kt) * P for kt in range(QT)}
        S_COL = {3: 0, 2: 512, 0: 896, 1: 1024}
        S_LEN = {qt: (qt + 1) * P for qt in range(QT)}

        block = ctx.enter_context(nc.Block())

        @block.sync
        def _(sp):
            def load(dst, src, signal):
                sp.dma_start(dst, src).then_inc(signal, 16)

            def rows(b):
                load(xs[:, b * QT:(b + 1) * QT, :], x[b].rearrange("(t p) d -> p t d", p=P), ld_x[b])

            def weight(j, w):
                load(wqkv[:, j, :, :], w.rearrange("(k p) n -> p k n", p=P), (ld_wq, ld_wk, ld_wv)[j])

            def context(b):
                load(ctxT_s[:, :, b, :], ctxT[b, :, 0:SQ].rearrange("(k p) s -> p k s", p=P), ld_ctx[b])

            rows(0)
            weight(1, wkT)
            context(0)
            weight(0, wqT)
            rows(1)
            context(1)
            weight(2, wvT)
            sp.wait_ge(consts, 3)
            for s in range(SLOTS):
                sp.dma_start(aug[KROWS:KROWS_M, s, 1, :, :], ones_row[:].rearrange("p (o t) -> p o t", o=1)
                             .to_broadcast([2, GH, SQ])).then_inc(ld_ones, 16)

            def part_out(kind, u, part):
                s = CUT_AT[(kind, u)]
                made = (pre_act, mid_done, low_done)[part]
                sp.wait_ge(made, s + 1 if part else PRE_AT[(kind, u)] + 1)
                sp.dma_start(scr[s, :, part, :, :], split[:, s, part, :]).then_inc(scr_done[s], 16)

            def stack(kind, g):
                u, h0 = g * GH // HU, g * GH % HU
                s, j = CUT_AT[(kind, u)], "qk".index(kind)
                sp.wait_ge(scr_done[s], 16 * 3)
                if g >= SLOTS:
                    sp.wait_ge(t_fill, 2 * GH * (g - SLOTS + 1))
                r0 = 0
                for run in (RUNS_Q, RUNS_K)[j]:
                    sp.dma_start(aug[r0:r0 + len(run) * HD, g % SLOTS, j, :, :],
                                 scr[s, h0:h0 + GH, 0:len(run), :, :].rearrange("h a d t -> (a d) h t")
                                 ).then_inc(aug_done[g % SLOTS], 16)
                    r0 += len(run) * HD

            def maxima(g):
                sp.wait_ge(misc_act, act_no(("mT", g)))
                for part in range(2):
                    sp.dma_start(aug[KROWS + part:KROWS + part + 1, g % SLOTS, 0, :, :],
                                 mrow[part * GH:(part + 1) * GH, g % 2, :]).then_inc(mdma_done[g % 2], 16)

            def load_w1(c):
                if c >= 1:
                    sp.wait_ge(w1l_done, c)
                for e in range(E):
                    sp.dma_start(w1f[:, e, :, :], w1[e, :, c * P:(c + 1) * P].rearrange(
                        "(k p) i -> p k i", p=P)).then_inc(ld_w1, 16)

            for step in SP_OPEN:
                if step[0] == "stack":
                    stack(*step[1:])
                elif step[0] == "maxima":
                    maxima(step[1])
                else:
                    part_out(*step)
            for r in range(GH):
                for a in range(2):
                    sp.dma_start(wo_att[BK * r + HD * a:BK * r + HD * (a + 1), :, :], woT.rearrange(
                        "(g a r d) n -> r a d g n", a=2, r=GH, d=HD)[r, a]).then_inc(ld_woT, 16)
            sp.dma_start(wo_s[:], wo.rearrange("(c p) n -> p c n", p=P)).then_inc(ld_wo, 16)
            for g in range(SLOTS, NG):
                stack("k", g)
                stack("q", g)
                maxima(g - 2)
                if g == SLOTS:
                    sp.wait_ge(pre_act, len(PRE))
                    load_w1(0)
                    sp.wait_ge(b1_zero, 1)
                    for r in (0, BK):
                        sp.dma_start(b1f[r:r + E, :], b1).then_inc(ld_b1, 16)
            maxima(NG - 2)
            load_w1(1)
            maxima(NG - 1)
            for c in range(2, IC):
                load_w1(c)

            for t in range(NT):
                sp.wait_ge(z_done, t + 1)
                sp.dma_start(out[t // QT, t % QT * P:(t % QT + 1) * P, :], xn[:, t, :]).then_inc(out_done, 16)
            sp.wait_ge(out_done, 16 * NT)

        @block.gpsimd
        def _(pool):
            nc.gpsimd.memset(mhalf[:], -0.5).then_inc(consts, 1)
            nc.gpsimd.memset(ones_sq[:], 1.0).then_inc(consts, 1)
            nc.gpsimd.memset(ones_row[:], 1.0).then_inc(consts, 1)
            pool.wait_ge(consts, 3)
            nc.gpsimd.affine_select(out=ident[:], in_=ones_sq[:], compare_op=ALU.is_equal, fill=0.0, base=0,
                                    pattern=[[-1, P]], channel_multiplier=1).then_inc(consts, 1)
            own = 0
            n_rows = 0

            def row_scale(which, t, eps):
                nonlocal own, n_rows
                n_rows += 1
                pool.wait_ge(stat_done, n_rows)
                nc.gpsimd.tensor_scalar(veps[:, which, t:t + 1], mv[:, which, t, 1:2], eps, None, ALU.add
                                        ).then_inc(pool_own, 1)
                own += 1
                pool.wait_ge(pool_own, own)
                nc.gpsimd.tensor_tensor(rstd[:, which, t:t + 1], veps[:, which, t:t + 1], mhalf[:], ALU.pow
                                        ).then_inc(rstd_done, 1)

            def low_part(job):
                s = CUT_AT[job]
                pool.wait_ge(mid_done, s + 1)
                nc.gpsimd.tensor_tensor(split[:, s, 2, :], rest[:, s % RS, :], split[:, s, 1, :],
                                        ALU.subtract).then_inc(low_done, 1)

            for t in range(QT):
                row_scale(0, t, LN_EPS)
            nc.gpsimd.memset(mask[:], 0.0).then_inc(pool_own, 1)
            own += 1
            pool.wait_ge(pool_own, own)
            nc.gpsimd.affine_select(out=mask[:, SQ - P:SQ], in_=mask[:, SQ - P:SQ], compare_op=ALU.is_ge, fill=NEG,
                                    base=0, pattern=[[-1, P]], channel_multiplier=1).then_inc(consts, 1)
            nc.gpsimd.affine_select(out=identb[:], in_=ones_sq[:], compare_op=ALU.is_equal, fill=0.0, base=0,
                                    pattern=[[-1, P]], channel_multiplier=1).then_inc(consts, 1)
            for t in range(QT, NT):
                row_scale(0, t, LN_EPS)
            low_part(("k", 0))
            low_part(("q", 0))
            nc.gpsimd.memset(vaug[:, :, H * VW:], 0.0).then_inc(consts, 1)
            nc.gpsimd.memset(vaug[:, :, 0:H * VW].rearrange("p t (h v) -> p t h v", v=VW)[:, :, :, HD:VW], 1.0
                             ).then_inc(consts, 1)
            for job in CUTS[2:]:
                low_part(job)
            for e in range(E):
                nc.gpsimd.memset(pri[:, e:e + 1], float(E - e)).then_inc(consts, 1)
            nc.gpsimd.memset(oh[:], 0.0).then_inc(consts, 1)
            nc.gpsimd.memset(picks[:], 1.0).then_inc(pool_own, 1)
            own += 1
            pool.wait_ge(pool_own, own)
            nc.gpsimd.affine_select(out=picks[:], in_=picks[:], compare_op=ALU.is_equal, fill=0.0, base=0,
                                    pattern=[[-1, E], [0, P]], channel_multiplier=1).then_inc(picks_done, 1)
            pool.dma_start(wr_s[:], w_router.rearrange("(k p) e -> p k e", p=P)).then_inc(ld_small, 16)
            pool.dma_start(gam[:], gamma[None, :].to_broadcast([P, D])).then_inc(ld_small, 16)
            pool.dma_start(bet[:], beta[None, :].to_broadcast([P, D])).then_inc(ld_small, 16)
            pool.dma_start(bo_s[:], bo[None, :].to_broadcast([P, D])).then_inc(ld_small, 16)
            pool.wait_ge(pre_act, len(PRE))
            nc.gpsimd.memset(b1f[:], 0.0).then_inc(b1_zero, 1)

            def causal(n):
                pool.wait_ge(t_free, 2 * n + 2)
                pt = pT[:, n % PR, :]
                three = pt.rearrange("p (a b) -> p a b", b=2 * P)[:, 0:5:2, 0:P]
                nc.gpsimd.affine_select(out=three, in_=three, compare_op=ALU.is_ge, fill=0.0, base=0,
                                        pattern=[[0, 3], [1, P]], channel_multiplier=-1)
                one = pt[:, T_COL[3]:T_COL[3] + P]
                nc.gpsimd.affine_select(out=one, in_=one, compare_op=ALU.is_ge, fill=0.0, base=0,
                                        pattern=[[1, P]], channel_multiplier=-1).then_inc(p_masked, 1)

            def masked(b):
                pool.wait_ge(x_parts, 2 * (b + 1))
                for e, part in XM_POOL[b]:
                    pool.wait_ge(misc_act, act_no(("mk", E * b + e)))
                    nc.gpsimd.tensor_tensor(xmT[b][part][:, e, :, :], xhl[b][part][:].bitcast(fp32), spread_mask(e),
                                            ALU.mult).then_inc(xm_pool, 1)

            def cut_low(c):
                pool.wait_ge(w1h_done, c + 1)
                nc.gpsimd.tensor_tensor(w1l[c % RW][:], w1f[:], w1h[c % RW][:].bitcast(fp32),
                                        ALU.subtract).then_inc(w1l_done, 1)

            def addends(b):
                t = slice(b * QT, (b + 1) * QT)
                for dst, src in ((xn, bo_s), (xs, bet)):
                    nc.gpsimd.tensor_tensor(dst[:, t, :], dst[:, t, :], src[:].rearrange(
                        "p (o d) -> p o d", o=1).to_broadcast([P, QT, D]), ALU.add).then_inc(xb_done, 1)

            for n in range(NH):
                for w in range(2):
                    if w == 1:
                        causal(n)
                    for kind, t in STEP_MISC[n, w]:
                        if kind == "x1":
                            row_scale(1, t, LN_EPS)
                            pool.wait_ge(rstd_done, NT + t + 1)
                            nc.gpsimd.tensor_scalar(xn[:, t, :], xs[:, t, :], mv[:, 1, t, 0:1], rstd[:, 1, t:t + 1],
                                                    ALU.subtract, ALU.mult).then_inc(xn_pool, 1)
                if n >= GH + NORM_AT and (n - NORM_AT) % GH == 0:
                    g = (n - NORM_AT) // GH - 1
                    pool.wait_ge(rsum_done, g + 1)
                    if g % 2 == 0 and g >= 2:
                        pool.wait_ge(on_done, g // 2)
                    nc.gpsimd.tensor_tensor(*scale_operands(g), ALU.mult).then_inc(scaled, 1)
                if n == POOL_W1[0]:
                    cut_low(0)
                if n == POOL_W1[1]:
                    cut_low(1)
                if n == POOL_M0:
                    masked(0)
            cut_low(2)
            for t in range(QT, NT):
                row_scale(1, t, LN_EPS)

            def cut_wo(k):
                c = slice(k * IC // 2, (k + 1) * IC // 2)
                pool.wait_ge(wo_high, 1)
                nc.gpsimd.tensor_tensor(wo_l[:, c, :], wo_s[:, c, :], wo_h[:, c, :].bitcast(fp32),
                                        ALU.subtract).then_inc(wo_low, 1)

            cut_wo(0)
            masked(1)
            cut_low(3)
            cut_wo(1)
            pool.wait_ge(ld_small, 16 * 4)
            pool.wait_ge(misc_fill, MISC_AT[("xT", NT - 1)] + 1)
            addends(0)
            addends(1)
            for c in range(4, IC):
                cut_low(c)
            for t in range(NT):
                row_scale(2, t, FFN_EPS)

        @block.scalar
        def _(act):
            def take_pre(job):
                kind, k = job
                i = PRE_AT[job]
                act.wait_ge(pre_fill, i + 1)
                bank = ps[:, PRE_BANK[i], :]
                if kind == "xT":
                    nc.scalar.copy(xnT[:, k // QT, :, k % QT * P:(k % QT + 1) * P], bank[:, 0:KC * P].rearrange(
                        "p (c t) -> p c t", c=KC)).then_inc(pre_act, 1)
                elif kind == "v":
                    act.wait_ge(consts, 8)
                    nc.scalar.copy(vaug[:, k, 0:H * VW].rearrange("p (h v) -> p h v", v=VW)[:, :, 0:HD],
                                   bank[:, 0:D].rearrange("p (h d) -> p h d", d=HD)).then_inc(pre_act, 1)
                else:
                    s = CUT_AT[job]
                    nc.scalar.activation(split[:, s, 0, :], bank, ACT.Copy,
                                         scale=SCALE if kind == "q" else 1.0).then_inc(pre_act, 1)

            def middle(job):
                s = CUT_AT[job]
                act.wait_ge(rest_done, s + 1)
                nc.scalar.copy(split[:, s, 1, :], rest[:, s % RS, :]).then_inc(mid_done, 1)

            def take_misc(job):
                kind, k = job
                bank = bank_of(job)
                act.wait_ge(misc_fill, MISC_AT[job] + 1)
                if kind == "mT":
                    if k >= 2:
                        act.wait_ge(mdma_done[k % 2], 32 * (k // 2))
                    nc.scalar.copy(mrow[:, k % 2, :], bank[0:2 * GH, 0:SQ // 2].bitcast(bf16)).then_inc(misc_act, 1)
                elif kind == "xT":
                    nc.scalar.copy(xnT[:, k // QT, :, k % QT * P:(k % QT + 1) * P], bank[:, 0:KC * P].rearrange(
                        "p (c t) -> p c t", c=KC)).then_inc(misc_act, 1)
                elif kind == "ohT":
                    nc.scalar.copy(ohT[:, k * SQ:(k + 1) * SQ], bank[0:OR, :]).then_inc(misc_act, 1)
                else:
                    if k >= E:
                        act.wait_ge(xm_dve, len(XM_DVE[0]))
                        act.wait_ge(xm_pool, len(XM_POOL[0]))
                    nc.scalar.copy(mk[:, k % E, :], bank).then_inc(misc_act, 1)

            def cut_w1(c):
                act.wait_ge(ld_w1, 16 * E * (c + 1))
                if c >= RW:
                    act.wait_ge(h_fill, UNIT_AT[(c - RW, 1)] + 1)
                nc.scalar.copy(w1h[c % RW][:], w1f[:]).then_inc(w1h_done, 1)

            late = None
            for job in PRE_A:
                take_pre(job)
                if late:
                    middle(late)
                late = job if job[0] in "kq" else None
            if late:
                middle(late)
            for n in range(LAG):
                for job in OPEN[n]:
                    take_pre(job)
                    if job[0] in "kq":
                        middle(job)
                for job in OPEN_MISC[n]:
                    take_misc(job)

            for n in range(STEPS):
                for job in STEP_MISC[n, 0]:
                    if job[0] in BY_ACT:
                        take_misc(job)
                if n < NH:
                    if n >= PR:
                        act.wait_ge(pv_done, (n - PR) // GH + 1)
                    act.wait_ge(t_fill, 2 * n + 1)
                    nc.scalar.activation(pT[:, n % PR, 0:512], ps[:, T0, :], ACT.Exp).then_inc(t_free, 1)
                    act.wait_ge(t_fill, 2 * n + 2)
                    nc.scalar.activation(pT[:, n % PR, 512:PCOLS], ps[:, T0 + 1:T0 + 3, :].rearrange(
                        "p a b -> p (a b)")[:, 0:PCOLS - 512], ACT.Exp).then_inc(t_free, 1)
                for job in STEP_MISC[n, 1]:
                    if job[0] in BY_ACT:
                        take_misc(job)
                if n == SEL_AT:
                    act.wait_ge(picks_done, 1)
                    nc.scalar.copy(sel[:], picks[:]).then_inc(sel_done, 1)
                if n == B1_AT:
                    act.wait_ge(ld_b1, 32)
                    nc.scalar.copy(b1s[:], b1f[:]).then_inc(b1_done, 1)
                if n == ACT_W1[0]:
                    cut_w1(0)
                if n == ACT_W1[1]:
                    cut_w1(1)

            def gelu(i, k=0):
                cols = slice(k * SQ // 2, (k + 1) * SQ // 2) if i == 2 * IC - 1 else slice(0, SQ)
                act.wait_ge(h_fill, i + k + 1)
                if i >= 2:
                    act.wait_ge(gl_done, i - 1)
                nc.scalar.activation(g_ring[:, i % 2, cols], ps[:, h_bank(i, k), cols], ACT.Gelu).then_inc(g_done, 1)

            gelu(0)
            act.wait_ge(pv_done, NG)
            cut_w1(2)
            act.wait_ge(ld_wo, 16)
            nc.scalar.copy(wo_h[:], wo_s[:]).then_inc(wo_high, 1)
            for job in LATE_B[:QT]:
                take_misc(job)
            gelu(1)
            for job in LATE_C + LATE_D:
                take_misc(job)
            for i in range(2, 2 * IC):
                gelu(i)
                c, half = UNITS[i]
                if half == 1 and c + RW < IC:
                    cut_w1(c + RW)
            gelu(2 * IC - 1, 1)

        @block.vector
        def _(dve):
            own = 0

            def stats_of(which, t, src):
                nonlocal own
                nc.vector.bn_stats(stats[:, which, t, :], src[:, t, :]).then_inc(dve_own, 1)
                own += 1
                dve.wait_ge(dve_own, own)
                nc.vector.bn_aggr(mv[:, which, t, :], stats[:, which, t, :]).then_inc(stat_done, 1)

            def normalise(which, src, t, signal):
                dve.wait_ge(rstd_done, which * NT + t + 1)
                nc.vector.tensor_scalar(xn[:, t, :], src[:, t, :], mv[:, which, t, 0:1], rstd[:, which, t:t + 1],
                                        ALU.subtract, ALU.mult).then_inc(signal, 1)

            def remainder(job):
                s = CUT_AT[job]
                dve.wait_ge(pre_act, PRE_AT[job] + 1)
                if s >= RS:
                    dve.wait_ge(low_done, s - RS + 1)
                nc.vector.scalar_tensor_tensor(out=rest[:, s % RS, :], in0=ps[:, PRE_BANK[PRE_AT[job]], :],
                                               scalar=SCALE if job[0] == "q" else 1.0, in1=split[:, s, 0, :],
                                               op0=ALU.mult, op1=ALU.subtract).then_inc(rest_done, 1)

            def stats_in(b):
                dve.wait_ge(ld_x[b], 16)
                for t in range(b * QT, (b + 1) * QT):
                    stats_of(0, t, xs)

            stats_in(0)
            for t in range(QT):
                normalise(0, xs, t, xn_done)
            stats_in(1)
            remainder(("k", 0))
            remainder(("q", 0))
            for t in range(QT, NT):
                normalise(0, xs, t, xn_done)
            for job in CUTS[2:6]:
                remainder(job)

            dve.wait_ge(consts, 5)

            def head_max(n):
                g, j = n // GH, n % GH
                for k, tiles in enumerate(((3,), (2, 0), (1,))):
                    dve.wait_ge(s_fill, 3 * n + k + 1)
                    for qt in tiles:
                        c = S_COL[qt]
                        scores = ps[:, S0 + c // 512, c % 512:c % 512 + S_LEN[qt]]
                        last = nc.vector.tensor_tensor_reduce(
                            out=scores, in0=scores, in1=mask[:, SQ - S_LEN[qt]:SQ], scale=1.0, scalar=NEG,
                            op0=ALU.add, op1=ALU.max, accum_out=mmax[:, g % 2, qt, j:j + 1])
                    last.then_inc(s_free, 1)
                if j == GH - 1:
                    if g >= 2:
                        dve.wait_ge(misc_fill, MISC_AT[("mT", g - 2)] + 1)
                    dve.wait_ge(s_free, 3 * n + 3)
                    nc.vector.tensor_scalar(mparts[:, g % 2, :, 0, :], mmax[:, g % 2, :, :], -1.0, None,
                                            ALU.mult).then_inc(m_high, 1)
                    dve.wait_ge(m_high, g + 1)
                    nc.vector.scalar_tensor_tensor(out=mparts[:, g % 2, :, 1, :], in0=mmax[:, g % 2, :, :],
                                                   scalar=-1.0, in1=mparts[:, g % 2, :, 0, :],
                                                   op0=ALU.mult, op1=ALU.subtract).then_inc(m_done, 1)

            def norm_sums(g):
                dve.wait_ge(pv_done, g + 1)
                if g >= 1:
                    dve.wait_ge(scaled, g)
                nc.vector.transpose(oq[:, 0, :, :].rearrange("p a b -> p (a b)"), ps[:, PO, :]).then_inc(o_taken, 1)
                dve.wait_ge(o_taken, g + 1)
                nc.vector.reciprocal(rsum[:], oq[:, 0, :, HD]).then_inc(rsum_done, 1)

            def norm_scale_last():
                g = NG - 1
                dve.wait_ge(rsum_done, g + 1)
                nc.vector.tensor_tensor(*scale_operands(g), ALU.mult).then_inc(scaled, 1)

            def norm_back(g):
                if g >= GB:
                    dve.wait_ge(misc_fill, MISC_AT[("x1", QT - 1)] + 1)
                dve.wait_ge(scaled, g + 1)
                nc.vector.transpose(onT[:, g % GB // 2, :], oq[:, 1, :, :].rearrange("p a b -> p (a b)")
                                    ).then_inc(on_done, 1)

            def one_hot(b, bank):
                ts = slice(b * QT, (b + 1) * QT)
                nc.vector.tensor_copy(lg[:, ts, :], bank[:, 0:QT * E].rearrange("p (t e) -> p t e", e=E)
                                      ).then_inc(misc_dve, 1)
                dve.wait_ge(misc_dve, dve_no(("logits", b)))

                def step(k):
                    dve.wait_ge(oh_step, 5 * b + k)

                def spread(m):
                    return m[:, ts].rearrange("p (t o) -> p t o", o=1).to_broadcast([P, QT, E])

                nc.vector.tensor_reduce(lmax[:, ts], lg[:, ts, :], mybir.AxisListType.X, ALU.max).then_inc(oh_step, 1)
                step(1)
                nc.vector.tensor_tensor(lg[:, ts, :], lg[:, ts, :], spread(lmax), ALU.is_equal).then_inc(oh_step, 1)
                step(2)
                nc.vector.tensor_tensor(lg[:, ts, :], lg[:, ts, :], pri[:].rearrange(
                    "p (o e) -> p o e", o=1).to_broadcast([P, QT, E]), ALU.mult).then_inc(oh_step, 1)
                step(3)
                nc.vector.tensor_reduce(lmax[:, ts], lg[:, ts, :], mybir.AxisListType.X, ALU.max).then_inc(oh_step, 1)
                step(4)
                nc.vector.tensor_tensor(oh[:, :, BK:BK + E], lg[:, ts, :], spread(lmax), ALU.is_equal)
                nc.vector.tensor_tensor(oh[:, :, 0:E], lg[:, ts, :], spread(lmax), ALU.is_equal).then_inc(oh_step, 1)

            def take_misc(job):
                kind, k = job
                bank = bank_of(job)
                dve.wait_ge(misc_fill, MISC_AT[job] + 1)
                if kind == "x1":
                    nc.vector.tensor_tensor(xs[:, k, :], xs[:, k, :], bank[:, 0:D], ALU.add).then_inc(misc_dve, 1)
                    dve.wait_ge(misc_dve, dve_no(job))
                    stats_of(1, k, xs)
                    if k < QT:
                        return
                    if k % QT:
                        normalise(1, xs, k - 1, xn_done)
                    if k % QT == QT - 1:
                        normalise(1, xs, k, xn_done)
                elif kind == "logits":
                    one_hot(k, bank)

            def cut_x(b, part):
                x_T, high = xnT[:, b, :, :], xhl[b][0]
                if part == 0:
                    if b:
                        dve.wait_ge(xm_dve, len(XM_DVE[0]))
                        dve.wait_ge(xm_pool, len(XM_POOL[0]))
                    dve.wait_ge(misc_act, act_no(("xT", b * QT + QT - 1)))
                    nc.vector.tensor_copy(high[:], x_T).then_inc(x_parts, 1)
                else:
                    dve.wait_ge(misc_fill, MISC_AT[("logits", b)] + 1)
                    dve.wait_ge(x_parts, 2 * b + 1)
                    nc.vector.tensor_tensor(xhl[b][1][:], x_T, high[:].bitcast(fp32), ALU.subtract
                                            ).then_inc(x_parts, 1)

            def masked(b):
                dve.wait_ge(x_parts, 2 * (b + 1))
                for e, part in XM_DVE[b]:
                    dve.wait_ge(misc_act, act_no(("mk", E * b + e)))
                    nc.vector.tensor_tensor(xmT[b][part][:, e, :, :], xhl[b][part][:].bitcast(fp32), spread_mask(e),
                                            ALU.mult).then_inc(xm_dve, 1)

            for n in range(LAG):
                head_max(n)
                for job in OPEN[n]:
                    if job[0] in "kq":
                        remainder(job)
            for n in range(STEPS):
                if n + LAG < NH:
                    head_max(n + LAG)
                g = (n - NORM_AT - BACK) // GH - 1
                if g >= 0 and (n - NORM_AT - BACK) % GH == 0 and g % 2 and g < NG - 1:
                    norm_back(g)
                for job in STEP_MISC[n, 0] + STEP_MISC[n, 1]:
                    if job[0] in BY_DVE:
                        take_misc(job)
                if n >= GH + NORM_AT and (n - NORM_AT) % GH == 0:
                    norm_sums((n - NORM_AT) // GH - 1)
                if n == B1_LOW_AT:
                    dve.wait_ge(b1_done, 1)
                    nc.vector.tensor_tensor(b1s[BK:2 * BK, :], b1f[BK:2 * BK, :], b1s[BK:2 * BK, :].bitcast(fp32),
                                            ALU.subtract).then_inc(b1_done, 1)
                for part in range(2):
                    if n == CUT_X_AT[part]:
                        cut_x(0, part)
                if n == DVE_M0:
                    masked(0)

            def cut_g(i, k=0):
                cols = slice(k * SQ // 2, (k + 1) * SQ // 2) if i == 2 * IC - 1 else slice(0, SQ)
                dve.wait_ge(g_done, i + k + 1)
                if i >= 2:
                    dve.wait_ge(y_done, QT * (i - 1))
                nc.vector.tensor_copy(g_h[:, i % 2, cols], g_ring[:, i % 2, cols]).then_inc(gh_done, 1)
                dve.wait_ge(gh_done, i + k + 1)
                nc.vector.tensor_tensor(g_l[:, i % 2, cols], g_ring[:, i % 2, cols],
                                        g_h[:, i % 2, cols].bitcast(fp32), ALU.subtract).then_inc(gl_done, 1)

            norm_sums(NG - 1)
            norm_scale_last()
            norm_back(NG - 1)
            cut_g(0)
            for job in LATE_A:
                take_misc(job)
            cut_x(1, 0)
            take_misc(("logits", 1))
            cut_x(1, 1)
            cut_g(1)
            masked(1)
            for i in range(2, END0 + 2):
                cut_g(i)

            dve.wait_ge(ld_small, 16 * 4)
            dve.wait_ge(xb_done, 2 * B)

            def last_stage(t):
                nonlocal own
                two = (t, t + 1)
                dve.wait_ge(y_done, QT * UNIT_AT[(IC - 1, t // QT)] + t % QT + 2)
                nc.vector.tensor_tensor(xn[:, t:t + 2, :], ps[:, 3 + t // 2, :].rearrange("p (t d) -> p t d", t=2),
                                        xn[:, t:t + 2, :], ALU.add).then_inc(dve_own, 1)
                own += 1
                dve.wait_ge(dve_own, own)
                for i in two:
                    nc.vector.bn_stats(stats[:, 2, i, :], xn[:, i, :]).then_inc(dve_own, 1)
                own += 2
                for i in two:
                    dve.wait_ge(dve_own, own - 1 + i - t)
                    nc.vector.bn_aggr(mv[:, 2, i, :], stats[:, 2, i, :]).then_inc(stat_done, 1)
                for i in two:
                    dve.wait_ge(stat_done, 2 * NT + i + 1)
                    nc.vector.scalar_tensor_tensor(out=xn[:, i, :], in0=xn[:, i, :], scalar=mv[:, 2, i, 0:1],
                                                   in1=gam[:], op0=ALU.subtract, op1=ALU.mult).then_inc(dve_own, 1)
                own += 2
                for i in two:
                    dve.wait_ge(dve_own, own - 1 + i - t)
                    dve.wait_ge(rstd_done, 2 * NT + i + 1)
                    nc.vector.scalar_tensor_tensor(out=xn[:, i, :], in0=xn[:, i, :], scalar=rstd[:, 2, i:i + 1],
                                                   in1=xs[:, i, :], op0=ALU.mult, op1=ALU.add).then_inc(z_done, 1)

            last_stage(0)
            cut_g(END0 + 2)
            last_stage(2)
            for i in range(END0 + 3, 2 * IC - 1):
                cut_g(i)
            for k in range(2):
                cut_g(2 * IC - 1, k)
            last_stage(QT)
            last_stage(QT + 2)

        @block.tensor
        def _(pe):
            def taken(jobs):
                for i in jobs:
                    if PRE[i][0] in "kq":
                        pe.wait_ge(rest_done, CUT_AT[PRE[i]] + 1)
                    else:
                        pe.wait_ge(pre_act, i + 1)

            def pre(job):
                kind, k = job
                i = PRE_AT[job]
                taken([b for b in range(i) if PRE_BANK[b] == PRE_BANK[i]][-1:])
                bank = ps[:, PRE_BANK[i], :]
                if kind == "xT":
                    pe.wait_ge(consts, 4)
                    pe.wait_ge(xn_done, k + 1)
                    for c in range(KC):
                        last = nc.tensor.transpose(bank[:, c * P:(c + 1) * P], xn[:, k, c * P:(c + 1) * P], ident[:])
                elif kind == "v":
                    pe.wait_ge(ld_wv, 16)
                    for c in range(KC):
                        last = nc.tensor.matmul(bank[:, 0:D], ctxT_s[:, c, k // QT, k % QT * P:(k % QT + 1) * P],
                                                wqkv[:, 2, c, :], start=(c == 0), stop=(c == KC - 1))
                else:
                    b, j = k // KC, "qk".index(kind)
                    if kind == "q":
                        pe.wait_ge(ld_wq, 16)
                        pe.wait_ge(pre_act, PRE_AT[("xT", b * QT + QT - 1)] + 1)
                    else:
                        pe.wait_ge(ld_wk, 16)
                        pe.wait_ge(ld_ctx[b], 16)
                    for c in range(KC):
                        src = ctxT_s[:, c, b, :] if kind == "k" else xnT[:, b, c, :]
                        last = nc.tensor.matmul(bank, wqkv[:, j, c, k % KC * P:(k % KC + 1) * P], src,
                                                start=(c == 0), stop=(c == KC - 1))
                last.then_inc(pre_fill, 1)

            def scores(n):
                g, h = n // GH, n % GH
                if h == 0:
                    pe.wait_ge(aug_done[g % SLOTS], 16 * (len(RUNS_Q) + len(RUNS_K)) * (g // SLOTS + 1))
                for k, tiles in enumerate(((3,), (2, 0), (1,))):
                    if n >= 1:
                        pe.wait_ge(s_free, 3 * (n - 1) + k + 1)
                    for qt in tiles:
                        c = S_COL[qt]
                        last = nc.tensor.matmul(ps[:, S0 + c // 512, c % 512:c % 512 + S_LEN[qt]],
                                                aug[0:KROWS, g % SLOTS, 0, h, qt * P:(qt + 1) * P],
                                                aug[0:KROWS, g % SLOTS, 1, h, 0:S_LEN[qt]], start=True, stop=True)
                    last.then_inc(s_fill, 1)

            def scores_T(n):
                g, h = n // GH, n % GH
                if h == 0:
                    pe.wait_ge(mdma_done[g % 2], 32 * (g // 2 + 1))
                for k, tiles in enumerate(((0,), (1, 3), (2,))):
                    if n >= 1 and k < 2:
                        pe.wait_ge(t_free, 2 * (n - 1) + k + 1)
                    for kt in tiles:
                        c = T_COL[kt]
                        last = nc.tensor.matmul(ps[:, T0 + c // 512, c % 512:c % 512 + T_LEN[kt]],
                                                aug[0:KROWS_M, g % SLOTS, 1, h, kt * P:(kt + 1) * P],
                                                aug[0:KROWS_M, g % SLOTS, 0, h, kt * P:SQ], start=True, stop=True)
                    if k != 1:
                        last.then_inc(t_fill, 1)

            def weigh(g, tiles):
                if tiles[0] == 0:
                    pe.wait_ge(p_masked, GH * (g + 1))
                    if g >= 1:
                        pe.wait_ge(o_taken, g)
                b = g // GB
                for kt in tiles:
                    for j in range(GH):
                        n = g * GH + j
                        v0 = n % H * VW
                        last = nc.tensor.matmul(ps[BK * j:BK * j + BK, PO, kt * P:SQ],
                                                vaug[:, b * QT + kt, v0:v0 + BK],
                                                pT[:, n % PR, T_COL[kt]:T_COL[kt] + T_LEN[kt]],
                                                start=(kt == 0), stop=(kt == QT - 1), skip_group_check=True)
                if tiles[-1] == QT - 1:
                    last.then_inc(pv_done, 1)

            def misc(job):
                kind, k = job
                i = MISC_AT[job]
                bank = bank_of(job)
                if MISC_BANK[i] < T0:
                    pe.wait_ge(s_free, 3 * NH)
                before = [m for m in MISC[:i] if MISC_BANK[MISC_AT[m]] == MISC_BANK[i]]
                if before:
                    if before[-1][0] in BY_DVE:
                        pe.wait_ge(misc_dve, dve_no(before[-1]))
                    else:
                        pe.wait_ge(misc_act, act_no(before[-1]))
                if kind == "mT":
                    pe.wait_ge(m_done, k + 1)
                    for qt in range(QT):
                        last = nc.tensor.transpose(bank[0:2 * GH, qt * P // 2:(qt + 1) * P // 2].bitcast(bf16),
                                                   mparts[:, k % 2, qt, :, :].rearrange("p a b -> p (a b)"),
                                                   identb[:])
                elif kind == "x1":
                    pe.wait_ge(on_done, GB // 2 * (k // QT + 1))
                    pe.wait_ge(ld_woT, 16 * 2 * GH)
                    for g in range(GB // 2):
                        last = nc.tensor.matmul(bank[:, 0:D], onT[:, g, k % QT * P:(k % QT + 1) * P],
                                                wo_att[:, g, :], start=(g == 0), stop=(g == GB // 2 - 1))
                elif kind == "xT":
                    if k < QT:
                        pe.wait_ge(xn_pool, k + 1)
                    else:
                        pe.wait_ge(xn_done, NT + k - QT + 1)
                    for c in range(KC):
                        last = nc.tensor.transpose(bank[:, c * P:(c + 1) * P], xn[:, k, c * P:(c + 1) * P], ident[:])
                elif kind == "logits":
                    pe.wait_ge(ld_small, 16 * 4)
                    pe.wait_ge(misc_act, act_no(("xT", k * QT + QT - 1)))
                    for t in range(k * QT, (k + 1) * QT):
                        for c in range(KC):
                            last = nc.tensor.matmul(bank[:, t % QT * E:(t % QT + 1) * E],
                                                    xnT[:, k, c, t % QT * P:(t % QT + 1) * P], wr_s[:, c, :],
                                                    start=(c == 0), stop=(c == KC - 1))
                elif kind == "ohT":
                    pe.wait_ge(oh_step, 5 * (k + 1))
                    for j in range(QT):
                        last = nc.tensor.transpose(bank[0:OR, j * P:(j + 1) * P], oh[:, j, :], ident[:])
                else:
                    b, e = k // E, k % E
                    pe.wait_ge(sel_done, 1)
                    pe.wait_ge(misc_act, act_no(("ohT", b)))
                    last = nc.tensor.matmul(bank, sel[:, e, :], ohT[:, b * SQ:(b + 1) * SQ], start=True, stop=True)
                last.then_inc(misc_fill, 1)

            for job in PRE_A:
                pre(job)
            for n in range(LAG):
                scores(n)
                for job in OPEN[n]:
                    pre(job)
                for job in OPEN_MISC[n]:
                    if job == MISC[0]:
                        pe.wait_ge(consts, 6)
                        taken(range(len(PRE_A)))
                    misc(job)
            pe.wait_ge(pre_act, len(PRE))
            pe.wait_ge(rest_done, 2 * NU)
            pe.wait_ge(ld_ones, 16 * SLOTS)
            def hidden(i, experts=range(E), k2=None):
                c, half = UNITS[i]
                if not experts:
                    return
                cols = slice(0, SQ) if k2 is None else slice(k2 * SQ // 2, (k2 + 1) * SQ // 2)
                bank = ps[:, h_bank(i, k2 or 0), cols]
                if experts[0] == 0:
                    pe.wait_ge(w1l_done, c + 1)
                    if i >= 3:
                        pe.wait_ge(g_done, i - 2 + (k2 or 0))
                    nc.tensor.matmul(bank, b1s[:, c * P:(c + 1) * P],
                                     ohT[:, half * SQ + cols.start:half * SQ + cols.stop], start=True, stop=False)
                high, low = w1h[c % RW], w1l[c % RW]
                for e in experts:
                    if c == 0:
                        for made, mine in ((xm_dve, XM_DVE), (xm_pool, XM_POOL)):
                            upto = [j for j, (ex, _) in enumerate(mine[half]) if ex == e]
                            if upto:
                                pe.wait_ge(made, half * len(mine[0]) + upto[-1] + 1)
                    for k in range(KC):
                        for w, part in ((high, 0), (low, 0), (high, 1)):
                            end = e == E - 1 and k == KC - 1 and part == 1
                            last = nc.tensor.matmul(bank, w[:, e, k, :], xmT[half][part][:, e, k, cols],
                                                    start=False, stop=end)
                if end:
                    last.then_inc(h_fill, 1)

            for n in range(STEPS):
                if n + LAG < NH:
                    scores(n + LAG)
                for job in STEP_MISC[n, 0]:
                    misc(job)
                if n < NH:
                    scores_T(n)
                for job in STEP_MISC[n, 1]:
                    misc(job)
                if n >= GH and WEIGH[n % GH]:
                    weigh(n // GH - 1, WEIGH[n % GH])
                for i, at_step in enumerate(HID_AT):
                    if n == at_step:
                        if i == 0:
                            pe.wait_ge(b1_done, 2)
                            pe.wait_ge(misc_act, act_no(("mk", E - 1)))
                        hidden(i // E, [i % E])

            def share(i):
                c, half = UNITS[i]
                pe.wait_ge(gl_done, i + 1)
                pe.wait_ge(wo_low, 1 if c < IC // 2 else 2)
                for j in range(QT):
                    if i == 2 * IC - 1 and j == QT // 2:
                        pe.wait_ge(gl_done, i + 2)
                    for g, w in ((g_h, wo_h), (g_l, wo_h), (g_h, wo_l)):
                        last = nc.tensor.matmul(ybank(half * QT + j), g[:, i % 2, j * P:(j + 1) * P], w[:, c, :],
                                                start=(c == 0 and j % 2 == 0 and w is wo_h and g is g_h),
                                                stop=(c == IC - 1 and w is wo_l), skip_group_check=True)
                    last.then_inc(y_done, 1)

            hidden(1, range(len(HID_AT) - E, max(len(HID_AT) - E, HID1_A)))
            pe.wait_ge(t_free, 2 * NH)
            pe.wait_ge(o_taken, NG)
            for job in LATE_A:
                misc(job)
            hidden(1, range(max(len(HID_AT) - E, HID1_A), E))
            for job in LATE_B:
                misc(job)
            share(0)
            hidden(2, range(0, 3))
            for job in LATE_C:
                misc(job)
            hidden(2, range(3, E))
            for job in LATE_D:
                misc(job)
            share(1)
            for i in range(3, 2 * IC - 1):
                hidden(i)
                share(i - 1)
            hidden(2 * IC - 1, k2=0)
            hidden(2 * IC - 1, k2=1)
            share(2 * IC - 2)
            share(2 * IC - 1)


def kernel(x, ctx_1024, L0_xattn_Wq, L0_xattn_Wk, L0_xattn_Wv, L0_xattn_Wo, L0_ffn_W_router, L0_ffn_W1, L0_ffn_b1,
           L0_ffn_Wo, L0_ffn_bo, L0_ffn_ln_gamma, L0_ffn_ln_beta):
    import numpy as np
    import concourse.bacc as bacc
    from concourse import mybir
    from concourse.bass_utils import run_bass_kernel_spmd

    laid = {
        "x": x, "ctxT": np.transpose(ctx_1024, (0, 2, 1)),
        "wqT": np.transpose(L0_xattn_Wq), "wkT": np.transpose(L0_xattn_Wk), "wvT": np.transpose(L0_xattn_Wv),
        "woT": np.transpose(L0_xattn_Wo), "w_router": L0_ffn_W_router, "w1": L0_ffn_W1, "b1": L0_ffn_b1,
        "wo": L0_ffn_Wo, "bo": L0_ffn_bo, "gamma": L0_ffn_ln_gamma, "beta": L0_ffn_ln_beta,
    }
    nc = bacc.Bacc("TRN2", target_bir_lowering=False, num_devices=1)
    arrays, aps = {}, []
    for name, a in laid.items():
        a = np.ascontiguousarray(a)
        arrays[f"in_{name}"] = a
        aps.append(nc.dram_tensor(f"in_{name}", a.shape, mybir.dt.from_np(a.dtype), kind="ExternalInput").ap())
    out = nc.dram_tensor("out_x", arrays["in_x"].shape, mybir.dt.float32, kind="ExternalOutput").ap()
    cross_attention_moe_ffn(nc, *aps, out)
    r = run_bass_kernel_spmd(nc, [arrays], core_ids=[0])
    return r.results[0]["out_x"]
```
